# Optimizing a Trainium2 kernel written in Bass

```python
import numpy as np
import jax
import jax.numpy as jnp

def _softmax(x, axis=-1):
    return jax.nn.softmax(x, axis=axis)

def _gelu(x):
    return jax.nn.gelu(x, approximate=True)

def _silu(x):
    return jax.nn.silu(x)

def _sigmoid(x):
    return jax.nn.sigmoid(x)

def _layernorm(x, axis=-1, eps=1e-05):
    m = jnp.mean(x, axis=axis, keepdims=True)
    v = jnp.var(x, axis=axis, keepdims=True)
    return (x - m) / jnp.sqrt(v + eps)

def _scatter_add(tgt, idx, src, axis=0):
    return tgt.at[idx].add(src)

def _segment_sum(src, seg, n):
    return jax.ops.segment_sum(src, seg, n)
kernel_name = 'mk_adj_preln_d1_adj_r2_118941'

def setup_inputs(seed: int=0):
    np.random.seed(seed)
    _w = jnp.asarray

    def _rec_inputs():
        import jax
        import jax.numpy as jnp
        _gk = jax.random.key(seed)
        x = -1.394e-06 + 0.9999 * jax.random.normal(jax.random.fold_in(_gk, 1), (64, 128, 256), jnp.float32)
        _w = (1.0 + jnp.arange(128, dtype=jnp.float32)) ** (-0.5)
        _w = _w / _w.mean()
        _pij = jnp.clip(0.03125 * _w[:, None] * _w[None, :], 0.0, 1.0)
        _a = jax.random.uniform(jax.random.fold_in(_gk, 2), (64, 128, 128)) < _pij
        adj = _a.astype(jnp.int32)
        return (x, adj)
    x, adj = _rec_inputs()

    def _L0_gnn_setup():
        import jax, jax.numpy as jnp
        import numpy as np
        NEG_INF = -1000000000.0
        NEG_SLOPE = 0.2

        def gat_layer(x, mask, W, a_src, a_dst, bias, concat):
            B, N, _ = x.shape
            H, F = a_src.shape
            xl = (x @ W).reshape(B, N, H, F)
            asrc = jnp.einsum('bnhf,hf->bnh', xl, a_src)
            adst = jnp.einsum('bnhf,hf->bnh', xl, a_dst)
            e = jax.nn.leaky_relu(asrc[:, :, None, :] + adst[:, None, :, :], NEG_SLOPE)
            e = jnp.where(mask[..., None], e, NEG_INF)
            attn = jax.nn.softmax(e, axis=1)
            out = jnp.einsum('bsdh,bshf->bdhf', attn, xl)
            if concat:
                out = out.reshape(B, N, H * F)
            else:
                out = out.mean(axis=2)
            return out + bias
        key = jax.random.key(seed)
        ks = jax.random.split(key, 10)
        B, N, Din, Fh, H, Dout = (8, 512, 256, 128, 4, 256)
        s = 0.05
        return {'adj': jax.random.randint(ks[0], (B, N, N), 0, 2, dtype=jnp.int32), 'x': jax.random.normal(ks[1], (B, N, Din), dtype=jnp.float32), 'W1': jax.random.normal(ks[2], (Din, H * Fh), dtype=jnp.float32) * s, 'att_src1': jax.random.normal(ks[3], (H, Fh), dtype=jnp.float32) * s, 'att_dst1': jax.random.normal(ks[4], (H, Fh), dtype=jnp.float32) * s, 'b1': jax.random.normal(ks[5], (H * Fh,), dtype=jnp.float32) * s, 'W2': jax.random.normal(ks[6], (H * Fh, Dout), dtype=jnp.float32) * s, 'att_src2': jax.random.normal(ks[7], (1, Dout), dtype=jnp.float32) * s, 'att_dst2': jax.random.normal(ks[8], (1, Dout), dtype=jnp.float32) * s, 'b2': jax.random.normal(ks[9], (Dout,), dtype=jnp.float32) * s}
    _L0_gnn_all = _L0_gnn_setup()
    _L0_gnn_in = {k: v for k, v in _L0_gnn_all.items() if k in ('W1', 'att_src1', 'att_dst1', 'b1', 'W2', 'att_src2', 'att_dst2', 'b2')}
    del _L0_gnn_all
    return {'x': x, 'adj': adj, 'L0_gnn_W1': _L0_gnn_in['W1'], 'L0_gnn_att_src1': _L0_gnn_in['att_src1'], 'L0_gnn_att_dst1': _L0_gnn_in['att_dst1'], 'L0_gnn_b1': _L0_gnn_in['b1'], 'L0_gnn_W2': _L0_gnn_in['W2'], 'L0_gnn_att_src2': _L0_gnn_in['att_src2'], 'L0_gnn_att_dst2': _L0_gnn_in['att_dst2'], 'L0_gnn_b2': _L0_gnn_in['b2']}

def reference(x, adj, L0_gnn_W1, L0_gnn_att_src1, L0_gnn_att_dst1, L0_gnn_b1, L0_gnn_W2, L0_gnn_att_src2, L0_gnn_att_dst2, L0_gnn_b2):
    import jax
    import jax.numpy as jnp

    def _L0_gnn_ref(adj, x, W1, att_src1, att_dst1, b1, W2, att_src2, att_dst2, b2):
        import jax, jax.numpy as jnp
        import numpy as np
        NEG_INF = -1000000000.0
        NEG_SLOPE = 0.2

        def gat_layer(x, mask, W, a_src, a_dst, bias, concat):
            B, N, _ = x.shape
            H, F = a_src.shape
            xl = (x @ W).reshape(B, N, H, F)
            asrc = jnp.einsum('bnhf,hf->bnh', xl, a_src)
            adst = jnp.einsum('bnhf,hf->bnh', xl, a_dst)
            e = jax.nn.leaky_relu(asrc[:, :, None, :] + adst[:, None, :, :], NEG_SLOPE)
            e = jnp.where(mask[..., None], e, NEG_INF)
            attn = jax.nn.softmax(e, axis=1)
            out = jnp.einsum('bsdh,bshf->bdhf', attn, xl)
            if concat:
                out = out.reshape(B, N, H * F)
            else:
                out = out.mean(axis=2)
            return out + bias
        B, N, _ = adj.shape
        mask = (adj > 0) | jnp.eye(N, dtype=bool)[None]
        h = jax.nn.elu(gat_layer(x, mask, W1, att_src1, att_dst1, b1, concat=True))
        h = gat_layer(h, mask, W2, att_src2, att_dst2, b2, concat=False)
        return h
    h = jnp.maximum(_layernorm(x, axis=-1), 0.0)
    x = x + _L0_gnn_ref(adj, h, L0_gnn_W1, L0_gnn_att_src1, L0_gnn_att_dst1, L0_gnn_b1, L0_gnn_W2, L0_gnn_att_src2, L0_gnn_att_dst2, L0_gnn_b2)
    return x

_drawn_inputs = setup_inputs


def setup_inputs(seed=0):
    import zlib

    import numpy as np

    out = dict(_drawn_inputs(seed))
    spreads = {}
    factors = {'L0_gnn_att_src1': 3.286,
     'L0_gnn_att_dst1': 8.0,
     'L0_gnn_att_src2': 4.494,
     'L0_gnn_att_dst2': 8.0}
    for name, (base, spread) in spreads.items():
        noise = np.random.default_rng([zlib.crc32(name.encode()), seed]).standard_normal(out[name].shape)
        drawn = base * np.exp(spread * noise) if base else spread * noise
        out[name] = jnp.asarray(drawn.astype(out[name].dtype))
    for name, factor in factors.items():
        out[name] = (out[name] * factor).astype(out[name].dtype)
    return out
```

```python
import concourse.bass as bass
from concourse import mybir
from contextlib import ExitStack


def preln_gat_residual_kernel(nc: bass.Bass, x, adj, W1, att_src1, att_dst1, b1, W2, att_src2, att_dst2, b2, out):
    fp32, bf16, i32 = mybir.dt.float32, mybir.dt.bfloat16, mybir.dt.int32
    ALU = mybir.AluOpType
    ACT = mybir.ActivationFunctionType
    AX = mybir.AxisListType

    NB, N, D = x.shape
    H, F = att_src1.shape
    DO = W2.shape[1]
    G = 4
    NG = NB // G
    KC = D // 128
    HALF = H // 2
    XW = HALF * F + H
    YW = DO + 2
    U = G * N
    NR = 24
    NEG = -float(2 ** 60)
    SLOPE = 0.2
    EPS = 1e-5
    assert H == G and N == 128 and F == 128 and D == 256 and DO == D

    ctx = ExitStack()
    with ctx:
        def sb(name, shape, dt=fp32):
            return ctx.enter_context(nc.sbuf_tensor(name, shape, dt))

        def pb(name, shape, dt=fp32):
            return ctx.enter_context(nc.psum_tensor(name, shape, dt))

        def sem(name):
            return ctx.enter_context(nc.semaphore(name))

        ident = sb("ident", [128, 128])
        ident_bf = sb("ident_bf", [128, 128], bf16)
        off_diag_neg = sb("off_diag_neg", [128, 128])
        pick_src = sb("pick_src", [NR, 4, 128], bf16)
        pick_dst = sb("pick_dst", [NR, 4, 128], bf16)
        pick_bias = sb("pick_bias", [68, H, N], bf16)
        w1 = sb("w1", [128, KC, 2, XW])
        w2 = sb("w2", [128, H, YW])
        a1_all = sb("a1_all", [128, 2, H, F])
        a2_all = sb("a2_all", [128, 2, DO])
        w_prod = sb("w_prod", [128, 2, 4, 256])
        b1_raw = sb("b1_raw", [68, F])
        b1_res = sb("b1_res", [68, 2, F])
        b1_part = sb("b1_part", [68, 3, F], bf16)
        b1_rows = sb("b1_rows", [68, F], bf16)
        b2_all = sb("b2_all", [128, DO])
        minus_half = sb("minus_half", [128, G])
        xs = sb("xs", [128, NB * D])
        adj_raw = sb("adj_raw", [128, 2, G, N], i32)
        neg_mask = sb("neg_mask", [128, 2, G, N], bf16)
        stats = sb("stats", [128, G, 6])
        mean_var = sb("mean_var", [128, 2, G, 2])
        var_eps = sb("var_eps", [128, G])
        rstd = sb("rstd", [128, 2, G])
        neg_mean = sb("neg_mean", [128, 2, G])
        hn = sb("hn", [128, 2, D])
        hT = sb("hT", [128, 2, KC, N])
        xl = sb("xl", [128, 4, 2, XW])
        cols_res = sb("cols_res", [128, 2, 2, 4])
        cols_part = sb("cols_part", [128, 2, 3, 2, 4], bf16)
        rows = sb("rows", [NR, 2, N], bf16)
        scaled = sb("scaled", [128, 2, U])
        z = sb("z", [128, 2, U])
        top = sb("top", [128, 2, 4])
        y = sb("y", [128, 2, U])
        e = sb("e", [128, 2, U])
        den = sb("den", [128, 2, 4])
        rden = sb("rden", [128, 2, 4])
        prob = sb("prob", [128, 2, U])
        probT = sb("probT", [128, 2, U])
        elu_exp = sb("elu_exp", [128, 2, U])
        elu_low = sb("elu_low", [128, 2, U])
        h1T = sb("h1T", [128, 2, U])
        xl2 = sb("xl2", [128, 2, G, YW])
        cols2_res = sb("cols2_res", [128, 2, 2, 4])
        cols2_part = sb("cols2_part", [128, 3, 2, 4], bf16)
        rows2 = sb("rows2", [NR, N], bf16)
        scaled2 = sb("scaled2", [128, U])
        z2 = sb("z2", [128, U])
        top2 = sb("top2", [128, 4])
        y2 = sb("y2", [128, U])
        e2 = sb("e2", [128, U])
        den2 = sb("den2", [128, 4])
        rden2 = sb("rden2", [128, 4])
        prob2 = sb("prob2", [128, U])
        prob2T = sb("prob2T", [128, U])
        result = sb("result", [128, 2, 2, DO])
        p_hT = pb("p_hT", [128, 512])
        p_xl = pb("p_xl", [128, 2, 512])
        p_score = pb("p_score", [128, 512])
        p_turn = pb("p_turn", [128, 512])
        p_o1 = pb("p_o1", [128, 512])
        p_xl2 = pb("p_xl2", [128, 512])
        p_o2 = pb("p_o2", [128, 512])
        p_rows = p_hT[:, 256:320].bitcast(bf16)
        p_rows2 = p_o2[:, 0:64].bitcast(bf16)

        S = {name: sem(name) for name in (
            "x_in0", "x_in1", "adj_in0", "adj_in1", "w1_in", "w2_in", "b1_in", "b2_in", "stored0", "stored1",
            "const_ready", "ident_ready", "pick_ready", "w1_prod", "w1_att", "w2_prod", "w2_att", "b1_step", "b1_ready",
            "stats_done", "mv_ready", "veps_done", "ln_ready", "hn_ready", "xb_ready", "mask_ready",
            "hT_done", "hT_ready", "xl_done", "xl_ready", "cols_step", "cols_ready", "rows_done", "rows_ready",
            "score_done", "scaled_ready", "z_ready", "top_ready", "y_ready", "e_ready", "den_done", "rden_ready",
            "prob_ready", "turn_done", "probT_ready", "o1_done", "eexp_ready", "elow_done", "h1T_ready",
            "xl2_done", "xl2_ready", "cols2_step", "cols2_ready", "rows2_done", "rows2_ready",
            "score2_done", "scaled2_ready", "z2_ready", "top2_ready", "y2_ready", "e2_ready", "den2_done",
            "rden2_ready", "prob2_ready", "turn2_done", "prob2T_ready", "o2_done", "result_ready")}

        def wait(eng, name, count):
            if not (isinstance(count, int) and count <= 0):
                eng.wait_ge(S[name], count)

        def held(eng, count):
            if not isinstance(count, int):
                eng.nop(nofuse=True)

        def graph(b):
            return not isinstance(b, int) or 0 <= b < NB

        def group(g):
            return not isinstance(g, int) or 0 <= g < NG

        def capped(v, top_value):
            return min(v, top_value) if isinstance(v, int) else v

        def per_slot(ap):
            return ap.unsqueeze(2).to_broadcast([128, 4, 128])

        def slots(ap):
            return ap.rearrange("p (a n) -> p a n", a=4)

        def run(eng, body):
            for i in (-1, 0, 1):
                body(i, i % 2, (i + 2) // 2 - 1)
            with eng.Fori(1, NG // 2 - 1) as r:
                body(2 * r, 0, r)
                body(2 * r + 1, 1, r)
            for i in range(NG - 2, NG + 2):
                body(i, i % 2, i // 2)

        block = ctx.enter_context(nc.Block())

        @block.sync
        def _(sp):
            def load_x(g, par):
                sp.dma_start(xs[:, bass.ds(g * G * D, G * D)].rearrange("p (b d) -> p b d", b=G),
                             x[bass.ds(g * G, G)].rearrange("b p d -> p b d")).then_inc(S[f"x_in{par}"], 16)

            def load_adj(g, par):
                sp.dma_start(adj_raw[:, par], adj[bass.ds(g * G, G)].rearrange("b s d -> s b d"))\
                  .then_inc(S[f"adj_in{par}"], 16)

            def body(i, par, r):
                if isinstance(i, int) and i == -1:
                    load_x(0, 0)
                    for c in range(KC):
                        for half in range(2):
                            sp.dma_start(w1[:, c, half, 0:HALF * F],
                                         W1[c * 128:(c + 1) * 128, half * HALF * F:(half + 1) * HALF * F])\
                              .then_inc(S["w1_in"], 16)
                    load_adj(0, 0)
                    load_x(1, 1)
                    load_adj(1, 1)
                    wait(sp, "b1_step", 1)
                    for p in range(3):
                        sp.dma_start(b1_raw[32 * p:32 * p + H, :], b1.rearrange("(h f) -> h f", h=H))\
                          .then_inc(S["b1_in"], 16)
                    sp.dma_start(w2[:, :, 0:DO], W2.rearrange("(h f) o -> f h o", h=H)).then_inc(S["w2_in"], 16)
                else:
                    if group(i + 2):
                        wait(sp, "stats_done", G * (i + 1))
                        load_x(i + 2, par)
                        wait(sp, "mask_ready", i + 1)
                        load_adj(i + 2, par)
                    j = i - 2
                    if group(j):
                        for pair in range(2):
                            wait(sp, "result_ready", 2 * j + pair + 1)
                            sp.dma_start(out[bass.ds(j * G + 2 * pair, 2)].rearrange("b p d -> p b d"),
                                         result[:, pair]).then_inc(S[f"stored{pair}"], 16)

            run(sp, body)
            wait(sp, "stored0", 16 * NG)
            wait(sp, "stored1", 16 * NG)

        @block.gpsimd
        def _(pool):
            count = {}

            def step(ins, name):
                count[name] = count.get(name, 0) + 1
                ins.then_inc(S[name], 1)
                pool.wait_ge(S[name], count[name])

            def setup():
                pool.memset(ident[:, :], 0.0).then_inc(S["const_ready"], 1)
                pool.memset(minus_half[:, :], -0.5).then_inc(S["const_ready"], 1)
                pool.memset(pick_src[:], 0.0).then_inc(S["const_ready"], 1)
                pool.memset(pick_dst[:], 0.0).then_inc(S["const_ready"], 1)
                pool.memset(pick_bias[:], 0.0).then_inc(S["const_ready"], 1)
                pool.memset(b1_rows[:], 0.0).then_inc(S["const_ready"], 1)
                pool.wait_ge(S["const_ready"], 6)
                pool.affine_select(out=ident[:, :], in_=ident[:, :], compare_op=ALU.not_equal, fill=1.0,
                                   base=0, pattern=[[-1, 128]], channel_multiplier=1).then_inc(S["ident_ready"], 1)
                pool.wait_ge(S["ident_ready"], 1)
                pool.tensor_copy(ident_bf[:, :], ident[:, :]).then_inc(S["ident_ready"], 1)
                pool.tensor_scalar(off_diag_neg[:, :], ident[:, :], -NEG, NEG, ALU.mult, ALU.add)\
                    .then_inc(S["ident_ready"], 1)
                n = 0
                for p in range(3):
                    for tile, first, per in ((pick_src, 0, 8), (pick_dst, 4, 8), (pick_bias, 0, 32)):
                        if n >= 3:
                            pool.wait_ge(S["pick_ready"], n - 2)
                        pool.affine_select(out=tile[:], in_=tile[:], compare_op=ALU.not_equal, fill=1.0,
                                           base=-(per * p + first), pattern=[[-1, 4], [0, 128]],
                                           channel_multiplier=1).then_inc(S["pick_ready"], 1)
                        n += 1

            def w1_products():
                pool.wait_ge(S["w1_in"], 16 * (2 * KC + 2))
                n = 0
                for c in range(KC):
                    for side in range(2):
                        if n >= 2:
                            pool.wait_ge(S["w1_att"], n - 1)
                        pool.tensor_tensor(w_prod[:, n % 2, 0:2, :], w1[:, c, :, 0:HALF * F],
                                           a1_all[:, side].rearrange("p (a b) f -> p a (b f)", a=2),
                                           ALU.mult).then_inc(S["w1_prod"], 1)
                        n += 1

            def w2_products():
                pool.wait_ge(S["w2_in"], 16 * 3)
                pool.wait_ge(S["w1_att"], 2 * KC)
                for side in range(2):
                    pool.tensor_tensor(w_prod[:, side], w2[:, :, 0:DO],
                                       a2_all[:, side].unsqueeze(1).to_broadcast([128, 4, DO]),
                                       ALU.mult).then_inc(S["w2_prod"], 1)

            def layernorm_terms(g, par):
                wait(pool, "mv_ready", G * (g + 1))
                wait(pool, "hn_ready", G * (g - 1))
                held(pool, g)
                pool.tensor_scalar(var_eps[:, :], mean_var[:, par, :, 1], EPS, 0.0, ALU.add, ALU.add)\
                    .then_inc(S["veps_done"], 1)
                wait(pool, "veps_done", g + 1)
                pool.tensor_tensor(rstd[:, par], var_eps[:, :], minus_half[:, :], ALU.pow)\
                    .then_inc(S["ln_ready"], 1)
                pool.tensor_scalar(neg_mean[:, par], mean_var[:, par, :, 0], -1.0, 0.0, ALU.mult, ALU.add)\
                    .then_inc(S["ln_ready"], 1)

            def residual_side(b):
                xb = xs[:, bass.ds(b * D, D)]
                if isinstance(b, int) and b == 0:
                    pool.wait_ge(S["b2_in"], 16)
                wait(pool, "hn_ready", b + 1)
                pool.tensor_tensor(xb, xb, b2_all[:, :], ALU.add).then_inc(S["xb_ready"], 1)

            def split(src, res, part, done, first, last_name):
                held(pool, done)
                pool.tensor_copy(part[:, 0], src).then_inc(S[first], 1)
                wait(pool, first, done + 1)
                pool.tensor_tensor(res[:, 0], src, part[:, 0], ALU.subtract).then_inc(S[first], 1)
                wait(pool, first, done + 2)
                held(pool, done)
                pool.tensor_copy(part[:, 1], res[:, 0]).then_inc(S[first], 1)
                wait(pool, first, done + 3)
                pool.tensor_tensor(part[:, 2], res[:, 0], part[:, 1], ALU.subtract).then_inc(S[last_name], 1)

            def subtract_top(dst, src, tops, name):
                pool.tensor_tensor(slots(dst), slots(src), per_slot(tops), ALU.subtract).then_inc(S[name], 1)

            def scale(dst, src, r, name):
                pool.tensor_tensor(slots(dst), slots(src), per_slot(r), ALU.mult).then_inc(S[name], 1)

            def body(i, par, r):
                if isinstance(i, int) and i == -1:
                    setup()
                for k in range(4):
                    t = 4 * i + k
                    j = i - 1
                    if k == 3 and group(j):
                        wait(pool, "xl2_ready", G * (j + 1))
                        wait(pool, "rows2_done", j)
                        split(xl2[:, 1 - par, :, DO:YW].rearrange("p b j -> p j b"), cols2_res[:], cols2_part[:],
                              3 * j, "cols2_step", "cols2_ready")
                    if graph(t - 1):
                        b = t - 1
                        wait(pool, "xl_ready", b + 1)
                        wait(pool, "rows_done", b - 1)
                        split(xl[:, (k - 1) % 4, :, HALF * F:XW], cols_res[:, 0:1].rearrange("p o a c -> p o a c"),
                              cols_part[:, (k - 1) % 2], 3 * b, "cols_step", "cols_ready")
                    if graph(t - 2):
                        b, q = t - 2, k % 2
                        wait(pool, "rden_ready", b + 1)
                        wait(pool, "turn_done", b - 1)
                        scale(prob[:, q], e[:, q], rden[:, q], "prob_ready")
                    if k == 0 and group(i - 2):
                        wait(pool, "rden2_ready", i - 1)
                        wait(pool, "turn2_done", i - 2)
                        scale(prob2[:, :], e2[:, :], rden2[:, :], "prob2_ready")
                    if k == 3 and group(i + 1):
                        layernorm_terms(i + 1, 1 - par)
                    if graph(t + 1):
                        residual_side(t + 1)
                    if graph(t - 1):
                        b, q = t - 1, (k - 1) % 2
                        wait(pool, "top_ready", b + 1)
                        wait(pool, "e_ready", b - 1)
                        subtract_top(y[:, q], z[:, q], top[:, q], "y_ready")
                    if k == 3 and group(j):
                        wait(pool, "top2_ready", j + 1)
                        wait(pool, "e2_ready", j)
                        subtract_top(y2[:, :], z2[:, :], top2[:, :], "y2_ready")
                if isinstance(i, int) and i == -1:
                    w1_products()
                    w2_products()

            run(pool, body)

        @block.scalar
        def _(act):
            for side, a in enumerate((att_src1, att_dst1)):
                act.dma_start(a1_all[:, side], a.partition_broadcast(128)).then_inc(S["w1_in"], 16)
            act.dma_start(b2_all[:, :], b2.partition_broadcast(128)).then_inc(S["b2_in"], 16)
            for side, a in enumerate((att_src2, att_dst2)):
                act.dma_start(a2_all[:, side], a.rearrange("a o -> (a o)").partition_broadcast(128))\
                   .then_inc(S["w2_in"], 16)

            def body(i, par, r):
                for k in range(4):
                    t = 4 * i + k
                    if graph(t):
                        wait(act, "hT_done", t + 1)
                        wait(act, "xl_done", t - 1)
                        act.activation(hT[:, k % 2], p_hT[:, 0:D].rearrange("p (c n) -> p c n", c=KC), ACT.Relu)\
                           .then_inc(S["hT_ready"], 1)
                    if k == 0 and group(i - 2):
                        wait(act, "y2_ready", i - 1)
                        wait(act, "prob2_ready", i - 2)
                        act.activation(e2[:, :], y2[:, :], ACT.Exp).then_inc(S["e2_ready"], 1)
                    if graph(t - 3):
                        b = t - 3
                        g = i + (k - 3) // 4
                        wait(act, "xl2_done", b + 1)
                        wait(act, "o2_done", 2 * (g - 1))
                        act.activation(xl2[:, (par + (k - 3) // 4) % 2, (k - 3) % 4, :], p_xl2[:, 0:YW], ACT.Copy)\
                           .then_inc(S["xl2_ready"], 1)
                    if graph(t - 1):
                        b, q = t - 1, (k - 1) % 2
                        wait(act, "rows_done", b + 1)
                        wait(act, "score_done", b - 1)
                        act.activation(rows[:, q], p_rows[0:NR, :], ACT.Copy).then_inc(S["rows_ready"], 1)
                    if k == 3 and group(i - 1):
                        wait(act, "rows2_done", i)
                        wait(act, "score2_done", i - 1)
                        act.activation(rows2[:, :], p_rows2[0:NR, :], ACT.Copy).then_inc(S["rows2_ready"], 1)
                    if graph(t - 2):
                        b, q = t - 2, k % 2
                        wait(act, "turn_done", b + 1)
                        wait(act, "o1_done", b - 1)
                        act.activation(probT[:, q], p_turn[:, :], ACT.Copy).then_inc(S["probT_ready"], 1)
                    if graph(t - 1):
                        b, q = t - 1, (k - 1) % 2
                        wait(act, "score_done", b + 1)
                        wait(act, "z_ready", b - 1)
                        act.activation(scaled[:, q], p_score[:, :], ACT.Copy, scale=SLOPE)\
                           .then_inc(S["scaled_ready"], 1)
                    if graph(t - 2):
                        b, q = t - 2, k % 2
                        wait(act, "o1_done", b + 1)
                        wait(act, "elow_done", b - 1)
                        act.activation(elu_exp[:, q], p_o1[:, :], ACT.Exp).then_inc(S["eexp_ready"], 1)
                    if graph(t):
                        wait(act, "xl_done", t + 1)
                        wait(act, "o1_done", t - 3)
                        act.activation(xl[:, k % 4], p_xl[:, :, 0:XW], ACT.Copy).then_inc(S["xl_ready"], 1)
                    if graph(t - 1):
                        b, q = t - 1, (k - 1) % 2
                        wait(act, "y_ready", b + 1)
                        wait(act, "prob_ready", b - 1)
                        act.activation(e[:, q], y[:, q], ACT.Exp).then_inc(S["e_ready"], 1)
                    if k == 3 and group(i - 1):
                        wait(act, "score2_done", i)
                        wait(act, "z2_ready", i - 1)
                        act.activation(scaled2[:, :], p_score[:, :], ACT.Copy, scale=SLOPE)\
                           .then_inc(S["scaled2_ready"], 1)
                    if k == 0 and group(i - 2):
                        wait(act, "turn2_done", i - 1)
                        wait(act, "o2_done", 2 * (i - 2))
                        act.activation(prob2T[:, :], p_turn[:, :], ACT.Copy).then_inc(S["prob2T_ready"], 1)

            run(act, body)

        @block.tensor
        def _(pe):
            def scores(bank_rows, mask_part, first_is_mask):
                if first_is_mask:
                    nc.tensor.matmul(p_score[:, :], mask_part, ident_bf[:, :].unsqueeze(1).to_broadcast([128, 4, 128]),
                                     start=True, stop=False)
                nc.tensor.matmul(p_score[:, :], bank_rows, pick_dst[:], start=not first_is_mask, stop=False)
                for a in range(4):
                    if not first_is_mask:
                        nc.tensor.matmul(p_score[:, a * 128:(a + 1) * 128], mask_part[:, a, :], ident_bf[:, :],
                                         start=False, stop=False)
                    mm = nc.tensor.matmul(p_score[:, a * 128:(a + 1) * 128], pick_src[:, a, :], bank_rows,
                                          start=False, stop=(a == 3))
                return mm

            def turn(src):
                for a in range(4):
                    mm = nc.tensor.transpose(p_turn[:, a * 128:(a + 1) * 128], src[:, a * 128:(a + 1) * 128], ident[:, :])
                return mm

            def body(i, par, r):
                if isinstance(i, int) and i == -1:
                    pe.wait_ge(S["ident_ready"], 3)
                    return
                for k in range(4):
                    t = 4 * i + k
                    if graph(t):
                        wait(pe, "hn_ready", t + 1)
                        wait(pe, "rows_ready", t - 1)
                        for c in range(KC):
                            mm = nc.tensor.transpose(p_hT[:, c * 128:(c + 1) * 128],
                                                     hn[:, k % 2, c * 128:(c + 1) * 128], ident[:, :])
                        mm.then_inc(S["hT_done"], 1)
                    if k in (1, 2) and group(i - 2):
                        j, pair = i - 2, k - 1
                        wait(pe, "prob2T_ready", j + 1)
                        wait(pe, "result_ready", 2 * j + pair)
                        for a in (2 * pair, 2 * pair + 1):
                            mm = nc.tensor.matmul(p_o2[:, (a % 2) * DO:(a % 2 + 1) * DO],
                                                  prob2T[:, a * 128:(a + 1) * 128], xl2[:, par, a, 0:DO],
                                                  start=True, stop=True)
                        mm.then_inc(S["o2_done"], 1)
                    if graph(t - 3):
                        b, q = t - 3, (k - 3) % 2
                        if isinstance(b, int) and b == 0:
                            pe.wait_ge(S["w2_att"], 2)
                        wait(pe, "h1T_ready", b + 1)
                        wait(pe, "xl2_ready", b)
                        for h in range(H):
                            mm = nc.tensor.matmul(p_xl2[:, 0:YW], h1T[:, q, h * 128:(h + 1) * 128], w2[:, h, :],
                                                  start=(h == 0), stop=(h == H - 1))
                        mm.then_inc(S["xl2_done"], 1)
                    if graph(t - 1):
                        b, q = t - 1, (k - 1) % 2
                        wait(pe, "cols_ready", b + 1)
                        wait(pe, "hT_ready", capped(t + 1, NB))
                        nc.tensor.transpose(p_rows[0:NR, :], cols_part[:, q].rearrange("p a b c -> p (a b c)"),
                                            ident_bf[:, :]).then_inc(S["rows_done"], 1)
                    if graph(t - 2):
                        b, q = t - 2, k % 2
                        wait(pe, "prob_ready", b + 1)
                        wait(pe, "probT_ready", b)
                        if k == 1 and group(i - 2):
                            wait(pe, "prob2T_ready", i - 1)
                        turn(prob[:, q]).then_inc(S["turn_done"], 1)
                    if k == 3 and group(i - 1):
                        wait(pe, "cols2_ready", i)
                        wait(pe, "result_ready", 2 * (i - 1))
                        nc.tensor.transpose(p_rows2[0:NR, :], cols2_part[:].rearrange("p a b c -> p (a b c)"),
                                            ident_bf[:, :]).then_inc(S["rows2_done"], 1)
                    if graph(t - 1):
                        b, q = t - 1, (k - 1) % 2
                        g = i + (k - 1) // 4
                        if isinstance(b, int) and b == 0:
                            pe.wait_ge(S["pick_ready"], 9)
                        wait(pe, "rows_ready", b + 1)
                        wait(pe, "mask_ready", g + 1)
                        wait(pe, "z_ready", b)
                        if k == 0 and group(i - 2):
                            wait(pe, "z2_ready", i - 1)
                        scores(rows[:, q], neg_mask[:, (par + (k - 1) // 4) % 2, (k - 1) % 4, :], True)\
                            .then_inc(S["score_done"], 1)
                    if graph(t - 2):
                        b, q = t - 2, k % 2
                        if isinstance(b, int) and b == 0:
                            pe.wait_ge(S["b1_ready"], 3)
                        wait(pe, "h1T_ready", b)
                        nc.tensor.matmul(p_o1[:, :], b1_rows[:, :], pick_bias[:], start=True, stop=False)
                        wait(pe, "probT_ready", b + 1)
                        wait(pe, "xl_ready", b + 1)
                        for h in range(H):
                            mm = nc.tensor.matmul(p_o1[:, h * 128:(h + 1) * 128],
                                                  xl[:, (k - 2) % 4, h // HALF, (h % HALF) * F:(h % HALF + 1) * F],
                                                  probT[:, q, h * 128:(h + 1) * 128], start=False, stop=(h == H - 1))
                        mm.then_inc(S["o1_done"], 1)
                    if graph(t):
                        if isinstance(t, int) and t == 0:
                            pe.wait_ge(S["w1_att"], 2 * KC)
                        wait(pe, "hT_ready", t + 1)
                        wait(pe, "xl_ready", t)
                        for half in range(2):
                            for c in range(KC):
                                mm = nc.tensor.matmul(p_xl[:, half, 0:XW], hT[:, k % 2, c, :], w1[:, c, half, :],
                                                      start=(c == 0), stop=(c == KC - 1))
                        mm.then_inc(S["xl_done"], 1)
                    if k == 3 and group(i - 1):
                        j = i - 1
                        wait(pe, "rows2_ready", j + 1)
                        wait(pe, "z_ready", capped(t, NB))
                        scores(rows2[:, :], neg_mask[:, 1 - par], False).then_inc(S["score2_done"], 1)
                    if k == 0 and group(i - 2):
                        wait(pe, "prob2_ready", i - 1)
                        wait(pe, "probT_ready", capped(t - 1, NB))
                        turn(prob2[:, :]).then_inc(S["turn2_done"], 1)

            run(pe, body)

        @block.vector
        def _(dve):
            def b1_parts():
                dve.wait_ge(S["b1_in"], 48)
                dve.tensor_copy(b1_part[:, 0], b1_raw[:, :]).then_inc(S["b1_step"], 1)
                dve.wait_ge(S["b1_step"], 2)
                dve.tensor_tensor(b1_res[:, 0], b1_raw[:, :], b1_part[:, 0], ALU.subtract).then_inc(S["b1_step"], 1)
                dve.wait_ge(S["b1_step"], 3)
                dve.tensor_copy(b1_part[:, 1], b1_res[:, 0]).then_inc(S["b1_step"], 1)
                dve.wait_ge(S["b1_step"], 4)
                dve.tensor_tensor(b1_part[:, 2], b1_res[:, 0], b1_part[:, 1], ALU.subtract).then_inc(S["b1_step"], 1)
                dve.wait_ge(S["b1_step"], 5)
                dve.wait_ge(S["const_ready"], 6)
                for p in range(3):
                    dve.tensor_copy(b1_rows[32 * p:32 * p + H, :], b1_part[32 * p:32 * p + H, p])\
                       .then_inc(S["b1_ready"], 1)

            def w1_columns():
                n = 0
                for c in range(KC):
                    for side in range(2):
                        dve.wait_ge(S["w1_prod"], n + 1)
                        dve.tensor_reduce(w1[:, c, side, HALF * F:XW],
                                          w_prod[:, n % 2, 0:2, :].rearrange("p a (b f) -> p (a b) f", f=F),
                                          AX.X, ALU.add).then_inc(S["w1_att"], 1)
                        n += 1

            def w2_columns():
                for side in range(2):
                    dve.wait_ge(S["w2_prod"], side + 1)
                    dve.tensor_reduce(w2[:, :, DO + side], w_prod[:, side], AX.X, ALU.add).then_inc(S["w2_att"], 1)

            def input_stats(b, par, c):
                dve.bn_stats(stats[:, c, :], xs[:, bass.ds(b * D, D)]).then_inc(S["stats_done"], 1)
                wait(dve, "stats_done", b + 1)
                held(dve, b)
                dve.bn_aggr(mean_var[:, par, c, :], stats[:, c, :]).then_inc(S["mv_ready"], 1)

            def normalise_input(b, g, par, c):
                wait(dve, "ln_ready", 2 * (g + 1))
                wait(dve, "hT_done", b - 1)
                dve.tensor_scalar(hn[:, c % 2], xs[:, bass.ds(b * D, D)], neg_mean[:, par, c:c + 1],
                                  rstd[:, par, c:c + 1], ALU.add, ALU.mult).then_inc(S["hn_ready"], 1)

            def leaky_and_top(scaled_t, z_t, top_t, z_name, top_name, z_count):
                dve.tensor_tensor(z_t, p_score[:, :], scaled_t, ALU.max).then_inc(S[z_name], 1)
                wait(dve, z_name, z_count)
                dve.tensor_reduce(top_t, slots(z_t), AX.X, ALU.max).then_inc(S[top_name], 1)

            def denominators(e_t, den_t, rden_t, den_name, rden_name, count):
                dve.tensor_reduce(den_t, slots(e_t), AX.X, ALU.add).then_inc(S[den_name], 1)
                wait(dve, den_name, count)
                dve.reciprocal(rden_t, den_t).then_inc(S[rden_name], 1)

            def body(i, par, r):
                if isinstance(i, int) and i == -1:
                    dve.memset(b1_raw[:, :], 0.0).then_inc(S["b1_step"], 1)
                for k in range(4):
                    t = 4 * i + k
                    if graph(t - 2):
                        b, q = t - 2, k % 2
                        wait(dve, "e_ready", b + 1)
                        wait(dve, "prob_ready", b - 1)
                        denominators(e[:, q], den[:, q], rden[:, q], "den_done", "rden_ready", b + 1)
                    for c in ((0, 1), (2,), (3,), ())[k]:
                        if group(i + 1):
                            g = i + 1
                            if c == 0:
                                wait(dve, f"x_in{1 - par}", 16 * (r + 1 + par))
                                wait(dve, "ln_ready", 2 * (g - 1))
                            wait(dve, "mv_ready", G * (g - 1) + c + 1)
                            input_stats(G * g + c, 1 - par, c)
                    if graph(t + 1):
                        normalise_input(t + 1, i + (k + 1) // 4, (par + (k + 1) // 4) % 2, (k + 1) % 4)
                    if k in (1, 2) and group(i - 2):
                        j, pair = i - 2, k - 1
                        wait(dve, "o2_done", 2 * j + pair + 1)
                        wait(dve, f"stored{pair}", 16 * j)
                        wait(dve, "xb_ready", G * j + 2 * pair + 2)
                        dve.tensor_tensor(result[:, pair].rearrange("p b d -> p (b d)"), p_o2[:, :],
                                          xs[:, bass.ds((G * j + 2 * pair) * D, 2 * D)], ALU.add)\
                           .then_inc(S["result_ready"], 1)
                    if k == 0 and group(i - 2):
                        wait(dve, "e2_ready", i - 1)
                        wait(dve, "prob2_ready", i - 2)
                        denominators(e2[:, :], den2[:, :], rden2[:, :], "den2_done", "rden2_ready", i - 1)
                    if isinstance(i, int) and i == -1 and k == 3:
                        w1_columns()
                    if k == 0 and group(i):
                        if isinstance(i, int) and i == 0:
                            dve.wait_ge(S["ident_ready"], 3)
                        wait(dve, f"adj_in{par}", 16 * (r + 1))
                        wait(dve, "score2_done", i - 1)
                        dve.scalar_tensor_tensor(out=neg_mask[:, par], in0=adj_raw[:, par], scalar=0.0,
                                                 in1=off_diag_neg[:, :].unsqueeze(1).to_broadcast([128, G, N]),
                                                 op0=ALU.is_le, op1=ALU.mult).then_inc(S["mask_ready"], 1)
                    if isinstance(i, int) and i == 0 and k == 0:
                        b1_parts()
                        w2_columns()
                    if graph(t - 1):
                        b, q = t - 1, (k - 1) % 2
                        wait(dve, "scaled_ready", b + 1)
                        wait(dve, "y_ready", b - 1)
                        leaky_and_top(scaled[:, q], z[:, q], top[:, q], "z_ready", "top_ready", b + 1)
                    if graph(t - 2):
                        b, q = t - 2, k % 2
                        wait(dve, "eexp_ready", b + 1)
                        wait(dve, "h1T_ready", b - 1)
                        dve.tensor_scalar(elu_low[:, q], elu_exp[:, q], 1.0, -1.0, ALU.min, ALU.add)\
                           .then_inc(S["elow_done"], 1)
                        wait(dve, "elow_done", b + 1)
                        wait(dve, "xl2_done", b - 1)
                        dve.tensor_tensor(h1T[:, q], p_o1[:, :], elu_low[:, q], ALU.max).then_inc(S["h1T_ready"], 1)
                    if k == 3 and group(i - 1):
                        j = i - 1
                        wait(dve, "scaled2_ready", j + 1)
                        wait(dve, "y2_ready", j)
                        leaky_and_top(scaled2[:, :], z2[:, :], top2[:, :], "z2_ready", "top2_ready", j + 1)

            run(dve, body)


_INS = ['x', 'adj', 'L0_gnn_W1', 'L0_gnn_att_src1', 'L0_gnn_att_dst1', 'L0_gnn_b1', 'L0_gnn_W2', 'L0_gnn_att_src2',
        'L0_gnn_att_dst2', 'L0_gnn_b2']
_OUTS = [((64, 128, 256), 'float32')]


def kernel(**inputs):
    import numpy as _np
    import concourse.bacc as _bacc
    from concourse import mybir as _mybir
    from concourse.bass_utils import run_bass_kernel_spmd as _run

    nc = _bacc.Bacc("TRN2", target_bir_lowering=False, num_devices=1)
    arrays, args = {}, []
    for name in _INS:
        a = _np.ascontiguousarray(inputs[name])
        arrays[f"in_{name}_dram"] = a
        args.append(nc.dram_tensor(f"in_{name}_dram", a.shape, _mybir.dt.from_np(a.dtype), kind="ExternalInput").ap())
    for i, (shape, dtype) in enumerate(_OUTS):
        dt = _mybir.dt.from_np(_np.dtype(dtype))
        args.append(nc.dram_tensor(f"out_{i}_dram", shape, dt, kind="ExternalOutput").ap())
    preln_gat_residual_kernel(nc, *args)
    r = _run(nc, [arrays], core_ids=[0])
    got = tuple(r.results[0][f"out_{i}_dram"] for i in range(len(_OUTS)))
    return got[0]
```

```python
import concourse.bass as bass
from concourse import mybir
from contextlib import ExitStack


def preln_gat_residual_kernel(nc: bass.Bass, x, adj, W1, att_src1, att_dst1, b1, W2, att_src2, att_dst2, b2, out):
    fp32, bf16, i32 = mybir.dt.float32, mybir.dt.bfloat16, mybir.dt.int32
    fp32r = mybir.dt.float32r
    ALU = mybir.AluOpType
    ACT = mybir.ActivationFunctionType
    AX = mybir.AxisListType

    NB, N, D = x.shape
    H, F = att_src1.shape
    DO = W2.shape[1]
    G = 4
    NG = NB // G
    KC = D // 128
    HALF = H // 2
    XW = HALF * F + H
    YW = DO + 2
    U = G * N
    NR = 24
    NEG = -float(2 ** 60)
    SLOPE = 0.2
    EPS = 1e-5
    assert H == G and N == 128 and F == 128 and D == 256 and DO == D

    ctx = ExitStack()
    with ctx:
        def sb(name, shape, dt=fp32):
            return ctx.enter_context(nc.sbuf_tensor(name, shape, dt))

        def pb(name, shape, dt=fp32):
            return ctx.enter_context(nc.psum_tensor(name, shape, dt))

        def sem(name):
            return ctx.enter_context(nc.semaphore(name))

        ident = sb("ident", [128, 128])
        ident_bf = sb("ident_bf", [128, 128], bf16)
        off_diag_neg = sb("off_diag_neg", [128, 128])
        pick_src = sb("pick_src", [NR, 4, 128], bf16)
        pick_dst = sb("pick_dst", [NR, 4, 128], bf16)
        pick_bias = sb("pick_bias", [68, H, N], bf16)
        w1 = sb("w1", [128, KC, 2, XW])
        w1_hi = sb("w1_hi", [128, KC, 2, XW], fp32r)
        w1_lo = sb("w1_lo", [128, KC, 2, XW], fp32r)
        w2 = sb("w2", [128, H, YW])
        w2_hi = sb("w2_hi", [128, H, YW], fp32r)
        w2_lo = sb("w2_lo", [128, H, YW], fp32r)
        a1_all = sb("a1_all", [128, 2, H, F])
        a2_all = sb("a2_all", [128, 2, DO])
        w_prod = sb("w_prod", [128, 2, 4, 256])
        b1_raw = sb("b1_raw", [68, F])
        b1_res = sb("b1_res", [68, 2, F])
        b1_part = sb("b1_part", [68, 3, F], bf16)
        b1_rows = sb("b1_rows", [68, F], bf16)
        b2_all = sb("b2_all", [128, DO])
        minus_half = sb("minus_half", [128, G])
        xs = sb("xs", [128, NB * D])
        adj_raw = sb("adj_raw", [128, 2, G, N], i32)
        neg_mask = sb("neg_mask", [128, 2, G, N], bf16)
        stats = sb("stats", [128, G, 6])
        mean_var = sb("mean_var", [128, 2, G, 2])
        var_eps = sb("var_eps", [128, G])
        rstd = sb("rstd", [128, 2, G])
        neg_mean = sb("neg_mean", [128, 2, G])
        hn = sb("hn", [128, 2, D])
        hT_hi = sb("hT_hi", [128, 2, KC, N], fp32r)
        hT_lo = sb("hT_lo", [128, 2, KC, N], fp32r)
        xl = sb("xl", [128, 4, 2, XW])
        cols_res = sb("cols_res", [128, 2, 2, 4])
        cols_part = sb("cols_part", [128, 2, 3, 2, 4], bf16)
        rows = sb("rows", [NR, 2, N], bf16)
        scaled = sb("scaled", [128, 2, U])
        z = sb("z", [128, 2, U])
        minus_top = sb("minus_top", [128, 2, 4])
        e = sb("e", [128, 2, U])
        den = sb("den", [128, 2, 4])
        rden = sb("rden", [128, 2, 4])
        prob = sb("prob", [128, 2, U])
        probT = sb("probT", [128, 2, U])
        elu_exp = sb("elu_exp", [128, 2, U])
        elu_low = sb("elu_low", [128, 2, U])
        h1T = sb("h1T", [128, 2, U])
        h1T_hi = sb("h1T_hi", [128, 2, U], fp32r)
        h1T_lo = sb("h1T_lo", [128, 2, U], fp32r)
        xl2 = sb("xl2", [128, 2, G, YW])
        cols2_res = sb("cols2_res", [128, 2, 2, 4])
        cols2_part = sb("cols2_part", [128, 3, 2, 4], bf16)
        rows2 = sb("rows2", [NR, N], bf16)
        scaled2 = sb("scaled2", [128, U])
        z2 = sb("z2", [128, U])
        minus_top2 = sb("minus_top2", [128, 4])
        e2 = sb("e2", [128, U])
        den2 = sb("den2", [128, 4])
        rden2 = sb("rden2", [128, 4])
        prob2 = sb("prob2", [128, U])
        prob2T = sb("prob2T", [128, U])
        result = sb("result", [128, 2, 2, DO])
        p_hT = pb("p_hT", [128, 512])
        p_xl = pb("p_xl", [128, 2, 512])
        p_score = pb("p_score", [128, 512])
        p_turn = pb("p_turn", [128, 512])
        p_o1 = pb("p_o1", [128, 512])
        p_xl2 = pb("p_xl2", [128, 512])
        p_o2 = pb("p_o2", [128, 512])
        p_rows = p_xl[:, 0, 448:512].bitcast(bf16)
        p_rows2 = p_xl[:, 1, 448:512].bitcast(bf16)

        S = {name: sem(name) for name in (
            "x_in0", "x_in1", "adj_in0", "adj_in1", "w1_in", "w2_in", "b1_in", "b2_in", "stored0", "stored1",
            "const_ready", "ident_ready", "pick_ready", "w1_prod", "w1_att", "w2_prod", "w2_att", "b1_step", "b1_ready",
            "stats_done", "mv_ready", "veps_done", "ln_ready", "hn_ready", "xb_ready", "mask_ready",
            "w1_hi_ready", "w1_lo_ready", "w2_hi_ready", "w2_lo_ready",
            "hT_done", "hT_hi_ready", "hT_lo_ready", "h1T_hi_ready", "h1T_lo_ready", "xl_done", "xl_ready", "cols_step", "cols_ready", "rows_done", "rows_ready",
            "score_done", "scaled_ready", "z_ready", "top_ready", "e_ready", "rden_ready",
            "prob_ready", "turn_done", "probT_ready", "o1_done", "eexp_ready", "elow_done", "h1T_ready",
            "xl2_done", "xl2_ready", "cols2_step", "cols2_ready", "rows2_done", "rows2_ready",
            "score2_done", "scaled2_ready", "z2_ready", "top2_ready", "e2_ready",
            "rden2_ready", "prob2_ready", "turn2_done", "prob2T_ready", "o2_done", "result_ready")}

        def wait(eng, name, count):
            if not (isinstance(count, int) and count <= 0):
                eng.wait_ge(S[name], count)

        def held(eng, count):
            if not isinstance(count, int):
                eng.nop(nofuse=True)

        def graph(b):
            return not isinstance(b, int) or 0 <= b < NB

        def group(g):
            return not isinstance(g, int) or 0 <= g < NG

        def capped(v, top_value):
            return min(v, top_value) if isinstance(v, int) else v

        def per_slot(ap):
            return ap.unsqueeze(2).to_broadcast([128, 4, 128])

        def slots(ap):
            return ap.rearrange("p (a n) -> p a n", a=4)

        def run(eng, body):
            for i in (-1, 0, 1):
                body(i, i % 2, (i + 2) // 2 - 1)
            with eng.Fori(1, NG // 2 - 1) as r:
                body(2 * r, 0, r)
                body(2 * r + 1, 1, r)
            for i in range(NG - 2, NG + 2):
                body(i, i % 2, i // 2)

        block = ctx.enter_context(nc.Block())

        @block.sync
        def _(sp):
            def load_x(g, par):
                sp.dma_start(xs[:, bass.ds(g * G * D, G * D)].rearrange("p (b d) -> p b d", b=G),
                             x[bass.ds(g * G, G)].rearrange("b p d -> p b d")).then_inc(S[f"x_in{par}"], 16)

            def load_adj(g, par):
                sp.dma_start(adj_raw[:, par], adj[bass.ds(g * G, G)].rearrange("b s d -> s b d"))\
                  .then_inc(S[f"adj_in{par}"], 16)

            def body(i, par, r):
                if isinstance(i, int) and i == -1:
                    load_x(0, 0)
                    for c in range(KC):
                        for half in range(2):
                            sp.dma_start(w1[:, c, half, 0:HALF * F],
                                         W1[c * 128:(c + 1) * 128, half * HALF * F:(half + 1) * HALF * F])\
                              .then_inc(S["w1_in"], 16)
                    load_adj(0, 0)
                    load_x(1, 1)
                    load_adj(1, 1)
                    wait(sp, "b1_step", 1)
                    for p in range(3):
                        sp.dma_start(b1_raw[32 * p:32 * p + H, :], b1.rearrange("(h f) -> h f", h=H))\
                          .then_inc(S["b1_in"], 16)
                    sp.dma_start(w2[:, :, 0:DO], W2.rearrange("(h f) o -> f h o", h=H)).then_inc(S["w2_in"], 16)
                else:
                    if group(i + 2):
                        wait(sp, "stats_done", G * (i + 1))
                        load_x(i + 2, par)
                        wait(sp, "mask_ready", i + 1)
                        load_adj(i + 2, par)
                    j = i - 2
                    if group(j):
                        for pair in range(2):
                            wait(sp, "result_ready", 2 * j + pair + 1)
                            sp.dma_start(out[bass.ds(j * G + 2 * pair, 2)].rearrange("b p d -> p b d"),
                                         result[:, pair]).then_inc(S[f"stored{pair}"], 16)

            run(sp, body)
            wait(sp, "stored0", 16 * NG)
            wait(sp, "stored1", 16 * NG)

        @block.gpsimd
        def _(pool):
            count = {}

            def step(ins, name):
                count[name] = count.get(name, 0) + 1
                ins.then_inc(S[name], 1)
                pool.wait_ge(S[name], count[name])

            def setup():
                pool.memset(ident[:, :], 0.0).then_inc(S["const_ready"], 1)
                pool.memset(minus_half[:, :], -0.5).then_inc(S["const_ready"], 1)
                pool.memset(pick_src[:], 0.0).then_inc(S["const_ready"], 1)
                pool.memset(pick_dst[:], 0.0).then_inc(S["const_ready"], 1)
                pool.memset(pick_bias[:], 0.0).then_inc(S["const_ready"], 1)
                pool.memset(b1_rows[:], 0.0).then_inc(S["const_ready"], 1)
                pool.wait_ge(S["const_ready"], 6)
                pool.affine_select(out=ident[:, :], in_=ident[:, :], compare_op=ALU.not_equal, fill=1.0,
                                   base=0, pattern=[[-1, 128]], channel_multiplier=1).then_inc(S["ident_ready"], 1)
                pool.wait_ge(S["ident_ready"], 1)
                pool.tensor_copy(ident_bf[:, :], ident[:, :]).then_inc(S["ident_ready"], 1)
                pool.tensor_scalar(off_diag_neg[:, :], ident[:, :], -NEG, NEG, ALU.mult, ALU.add)\
                    .then_inc(S["ident_ready"], 1)
                n = 0
                for p in range(3):
                    for tile, first, per in ((pick_src, 0, 8), (pick_dst, 4, 8), (pick_bias, 0, 32)):
                        if n >= 3:
                            pool.wait_ge(S["pick_ready"], n - 2)
                        pool.affine_select(out=tile[:], in_=tile[:], compare_op=ALU.not_equal, fill=1.0,
                                           base=-(per * p + first), pattern=[[-1, 4], [0, 128]],
                                           channel_multiplier=1).then_inc(S["pick_ready"], 1)
                        n += 1

            def w1_products():
                pool.wait_ge(S["w1_in"], 16 * (2 * KC + 2))
                n = 0
                for c in range(KC):
                    for side in range(2):
                        if n >= 2:
                            pool.wait_ge(S["w1_att"], n - 1)
                        pool.tensor_tensor(w_prod[:, n % 2, 0:2, :], w1[:, c, :, 0:HALF * F],
                                           a1_all[:, side].rearrange("p (a b) f -> p a (b f)", a=2),
                                           ALU.mult).then_inc(S["w1_prod"], 1)
                        n += 1

            def w2_products():
                pool.wait_ge(S["w2_in"], 16 * 3)
                pool.wait_ge(S["w1_att"], 2 * KC)
                for side in range(2):
                    pool.tensor_tensor(w_prod[:, side], w2[:, :, 0:DO],
                                       a2_all[:, side].unsqueeze(1).to_broadcast([128, 4, DO]),
                                       ALU.mult).then_inc(S["w2_prod"], 1)

            def layernorm_terms(g, par):
                wait(pool, "mv_ready", G * (g + 1))
                wait(pool, "hn_ready", G * (g - 1))
                held(pool, g)
                pool.tensor_scalar(var_eps[:, :], mean_var[:, par, :, 1], EPS, 0.0, ALU.add, ALU.add)\
                    .then_inc(S["veps_done"], 1)
                wait(pool, "veps_done", g + 1)
                pool.tensor_tensor(rstd[:, par], var_eps[:, :], minus_half[:, :], ALU.pow)\
                    .then_inc(S["ln_ready"], 1)
                pool.tensor_scalar(neg_mean[:, par], mean_var[:, par, :, 0], -1.0, 0.0, ALU.mult, ALU.add)\
                    .then_inc(S["ln_ready"], 1)

            def residual_side(b):
                xb = xs[:, bass.ds(b * D, D)]
                if isinstance(b, int) and b == 0:
                    pool.wait_ge(S["b2_in"], 16)
                wait(pool, "hn_ready", b + 1)
                pool.tensor_tensor(xb, xb, b2_all[:, :], ALU.add).then_inc(S["xb_ready"], 1)

            def split(src, res, part, done, first, last_name):
                held(pool, done)
                pool.tensor_copy(part[:, 0], src).then_inc(S[first], 1)
                wait(pool, first, done + 1)
                pool.tensor_tensor(res[:, 0], src, part[:, 0], ALU.subtract).then_inc(S[first], 1)
                wait(pool, first, done + 2)
                held(pool, done)
                pool.tensor_copy(part[:, 1], res[:, 0]).then_inc(S[first], 1)
                wait(pool, first, done + 3)
                pool.tensor_tensor(part[:, 2], res[:, 0], part[:, 1], ALU.subtract).then_inc(S[last_name], 1)

            def scale(dst, src, r, name):
                pool.tensor_tensor(slots(dst), slots(src), per_slot(r), ALU.mult).then_inc(S[name], 1)

            def body(i, par, r):
                if isinstance(i, int) and i == -1:
                    setup()
                for k in range(4):
                    t = 4 * i + k
                    if k == 3 and group(i - 1):
                        wait(pool, "xl2_ready", G * i)
                        wait(pool, "rows2_done", i - 1)
                        split(xl2[:, 1 - par, :, DO:YW].rearrange("p b j -> p j b"), cols2_res[:], cols2_part[:],
                              3 * (i - 1), "cols2_step", "cols2_ready")
                    if graph(t - 3):
                        b, q = t - 3, (k - 3) % 2
                        wait(pool, "h1T_hi_ready", b + 1)
                        wait(pool, "xl2_done", b - 1)
                        pool.tensor_tensor(h1T_lo[:, q], h1T[:, q], h1T_hi[:, q].bitcast(fp32), ALU.subtract)\
                            .then_inc(S["h1T_lo_ready"], 1)
                    if graph(t):
                        wait(pool, "xl_ready", t + 1)
                        wait(pool, "rows_done", t - 1)
                        split(xl[:, k, :, HALF * F:XW], cols_res[:, 0:1], cols_part[:, k % 2],
                              3 * t, "cols_step", "cols_ready")
                    if k == 1 and group(i - 2):
                        wait(pool, "rden2_ready", i - 1)
                        wait(pool, "turn2_done", i - 2)
                        scale(prob2[:, :], e2[:, :], rden2[:, :], "prob2_ready")
                    if graph(t + 1):
                        residual_side(t + 1)
                    if graph(t - 1):
                        b, q = t - 1, (k - 1) % 2
                        wait(pool, "rden_ready", b + 1)
                        wait(pool, "turn_done", b - 1)
                        scale(prob[:, q], e[:, q], rden[:, q], "prob_ready")
                    if k == 2 and group(i + 1):
                        layernorm_terms(i + 1, 1 - par)
                if isinstance(i, int) and i == -1:
                    w1_products()
                    w2_products()

            run(pool, body)

        @block.scalar
        def _(act):
            for side, a in enumerate((att_src1, att_dst1)):
                act.dma_start(a1_all[:, side], a.partition_broadcast(128)).then_inc(S["w1_in"], 16)
            act.dma_start(b2_all[:, :], b2.partition_broadcast(128)).then_inc(S["b2_in"], 16)
            for side, a in enumerate((att_src2, att_dst2)):
                act.dma_start(a2_all[:, side], a.rearrange("a o -> (a o)").partition_broadcast(128))\
                   .then_inc(S["w2_in"], 16)

            def exponentials(e_t, z_t, minus_top_t, den_t):
                for a in range(4):
                    at = slice(a * 128, (a + 1) * 128)
                    last = act.activation(e_t[:, at], z_t[:, at], ACT.Exp, bias=minus_top_t[:, a:a + 1],
                                          accum_out=den_t[:, a:a + 1])
                return last

            def body(i, par, r):
                for k in range(4):
                    t = 4 * i + k
                    if graph(t - 4):
                        b = t - 4
                        g = i - 1
                        wait(act, "xl2_done", b + 1)
                        wait(act, "o2_done", 2 * (g - 1))
                        act.activation(xl2[:, 1 - par, k, :], p_xl2[:, 0:YW], ACT.Copy).then_inc(S["xl2_ready"], 1)
                    if graph(t - 1):
                        b, q = t - 1, (k - 1) % 2
                        wait(act, "score_done", b + 1)
                        wait(act, "z_ready", b - 1)
                        act.activation(scaled[:, q], p_score[:, :], ACT.Copy, scale=SLOPE)\
                           .then_inc(S["scaled_ready"], 1)
                    if k == 0 and group(i - 2):
                        wait(act, "score2_done", i - 1)
                        wait(act, "z2_ready", i - 2)
                        act.activation(scaled2[:, :], p_o2[:, :], ACT.Copy, scale=SLOPE)\
                           .then_inc(S["scaled2_ready"], 1)
                    if graph(t):
                        wait(act, "xl_done", t + 1)
                        wait(act, "o1_done", t - 3)
                        act.activation(xl[:, k], p_xl[:, :, 0:XW], ACT.Copy).then_inc(S["xl_ready"], 1)
                    if graph(t - 2):
                        b, q = t - 2, k % 2
                        wait(act, "turn_done", b + 1)
                        wait(act, "o1_done", b - 1)
                        act.activation(probT[:, q], p_turn[:, :], ACT.Copy).then_inc(S["probT_ready"], 1)
                    if graph(t + 1):
                        wait(act, "hT_done", t + 2)
                        wait(act, "xl_done", t)
                        act.activation(hT_hi[:, (k + 1) % 2], p_hT[:, 0:D].rearrange("p (c n) -> p c n", c=KC), ACT.Relu)\
                           .then_inc(S["hT_hi_ready"], 1)
                    if graph(t - 1):
                        b, q = t - 1, (k - 1) % 2
                        wait(act, "top_ready", b + 1)
                        wait(act, "prob_ready", b - 1)
                        exponentials(e[:, q], z[:, q], minus_top[:, q], den[:, q]).then_inc(S["e_ready"], 1)
                    if graph(t - 2):
                        b, q = t - 2, k % 2
                        wait(act, "o1_done", b + 1)
                        wait(act, "elow_done", b - 1)
                        act.activation(elu_exp[:, q], p_o1[:, :], ACT.Exp).then_inc(S["eexp_ready"], 1)
                    if graph(t):
                        wait(act, "rows_done", t + 1)
                        wait(act, "score_done", t - 1)
                        act.activation(rows[:, k % 2], p_rows[0:NR, :], ACT.Copy).then_inc(S["rows_ready"], 1)
                    if k == 3 and group(i - 1):
                        wait(act, "rows2_done", i)
                        wait(act, "score2_done", i - 1)
                        act.activation(rows2[:, :], p_rows2[0:NR, :], ACT.Copy).then_inc(S["rows2_ready"], 1)
                    if k == 0 and group(i - 2):
                        wait(act, "top2_ready", i - 1)
                        wait(act, "prob2_ready", i - 2)
                        exponentials(e2[:, :], z2[:, :], minus_top2[:, :], den2[:, :]).then_inc(S["e2_ready"], 1)
                    if k == 1 and group(i - 2):
                        wait(act, "turn2_done", i - 1)
                        wait(act, "o2_done", 2 * (i - 2))
                        act.activation(prob2T[:, :], p_turn[:, :], ACT.Copy).then_inc(S["prob2T_ready"], 1)

            run(act, body)

        @block.tensor
        def _(pe):
            def scores(bank, bank_rows, mask_part, first_is_mask):
                if first_is_mask:
                    nc.tensor.matmul(bank[:, :], mask_part, ident_bf[:, :].unsqueeze(1).to_broadcast([128, 4, 128]),
                                     start=True, stop=False)
                nc.tensor.matmul(bank[:, :], bank_rows, pick_dst[:], start=not first_is_mask, stop=False)
                for a in range(4):
                    if not first_is_mask:
                        nc.tensor.matmul(bank[:, a * 128:(a + 1) * 128], mask_part[:, a, :], ident_bf[:, :],
                                         start=False, stop=False)
                    mm = nc.tensor.matmul(bank[:, a * 128:(a + 1) * 128], pick_src[:, a, :], bank_rows,
                                          start=False, stop=(a == 3))
                return mm

            def project1(hi, lo):
                for c in range(KC):
                    for n, (h_t, w) in enumerate(((hi, w1_hi), (hi, w1_lo), (lo, w1_hi))):
                        for half in range(2):
                            mm = nc.tensor.matmul(p_xl[:, half, 0:XW], h_t[:, c, :], w[:, c, half, :],
                                                  start=(c == 0 and n == 0), stop=(c == KC - 1 and n == 2))
                return mm

            def project2(hi, lo, heads):
                for h in heads:
                    for n, (h_t, w) in enumerate(((hi, w2_hi), (hi, w2_lo), (lo, w2_hi))):
                        mm = nc.tensor.matmul(p_xl2[:, 0:YW], h_t[:, h * 128:(h + 1) * 128], w[:, h, :],
                                              start=(h == 0 and n == 0), stop=(h == H - 1 and n == 2))
                return mm

            def turn(src):
                for a in range(4):
                    mm = nc.tensor.transpose(p_turn[:, a * 128:(a + 1) * 128], src[:, a * 128:(a + 1) * 128], ident[:, :])
                return mm

            def body(i, par, r):
                if isinstance(i, int) and i == -1:
                    pe.wait_ge(S["ident_ready"], 3)
                for k in range(4):
                    t = 4 * i + k
                    if graph(t - 1):
                        b, q = t - 1, (k - 1) % 2
                        g = i + (k - 1) // 4
                        if isinstance(b, int) and b == 0:
                            pe.wait_ge(S["pick_ready"], 9)
                        wait(pe, "rows_ready", b + 1)
                        wait(pe, "mask_ready", g + 1)
                        wait(pe, "z_ready", b)
                        scores(p_score, rows[:, q], neg_mask[:, (par + (k - 1) // 4) % 2, (k - 1) % 4, :], True)\
                            .then_inc(S["score_done"], 1)
                    if graph(t):
                        if isinstance(t, int) and t == 0:
                            pe.wait_ge(S["w1_lo_ready"], 1)
                        wait(pe, "hT_lo_ready", t + 1)
                        wait(pe, "rows_ready", t)
                        project1(hT_hi[:, k % 2], hT_lo[:, k % 2]).then_inc(S["xl_done"], 1)
                    if graph(t - 2):
                        b, q = t - 2, k % 2
                        wait(pe, "prob_ready", b + 1)
                        wait(pe, "probT_ready", b)
                        if k == 2 and group(i - 2):
                            wait(pe, "prob2T_ready", i - 1)
                        turn(prob[:, q]).then_inc(S["turn_done"], 1)
                    if graph(t + 1):
                        wait(pe, "hn_ready", t + 2)
                        wait(pe, "hT_lo_ready", t + 1)
                        for c in range(KC):
                            mm = nc.tensor.transpose(p_hT[:, c * 128:(c + 1) * 128],
                                                     hn[:, (k + 1) % 2, c * 128:(c + 1) * 128], ident[:, :])
                        mm.then_inc(S["hT_done"], 1)
                    if k in (2, 3) and group(i - 2):
                        j, pair = i - 2, k - 2
                        wait(pe, "prob2T_ready", j + 1)
                        wait(pe, "result_ready", 2 * j + pair)
                        for a in (2 * pair, 2 * pair + 1):
                            mm = nc.tensor.matmul(p_o2[:, (a % 2) * DO:(a % 2 + 1) * DO],
                                                  prob2T[:, a * 128:(a + 1) * 128], xl2[:, par, a, 0:DO],
                                                  start=True, stop=True)
                        mm.then_inc(S["o2_done"], 1)
                    if graph(t - 2):
                        b, q = t - 2, k % 2
                        if isinstance(b, int) and b == 0:
                            pe.wait_ge(S["b1_ready"], 3)
                        wait(pe, "h1T_ready", b)
                        nc.tensor.matmul(p_o1[:, :], b1_rows[:, :], pick_bias[:], start=True, stop=False)
                        wait(pe, "probT_ready", b + 1)
                        wait(pe, "xl_ready", b + 1)
                        for h in range(H):
                            mm = nc.tensor.matmul(p_o1[:, h * 128:(h + 1) * 128],
                                                  xl[:, (k - 2) % 4, h // HALF, (h % HALF) * F:(h % HALF + 1) * F],
                                                  probT[:, q, h * 128:(h + 1) * 128], start=False, stop=(h == H - 1))
                        mm.then_inc(S["o1_done"], 1)
                    if graph(t - 3):
                        b, q = t - 3, (k - 3) % 2
                        if isinstance(b, int) and b == 0:
                            pe.wait_ge(S["w2_lo_ready"], 1)
                        wait(pe, "h1T_lo_ready", b + 1)
                        wait(pe, "xl2_ready", b)
                        project2(h1T_hi[:, q], h1T_lo[:, q], (0, 1))
                    if graph(t):
                        wait(pe, "cols_ready", t + 1)
                        nc.tensor.transpose(p_rows[0:NR, :], cols_part[:, k % 2].rearrange("p a b c -> p (a b c)"),
                                            ident_bf[:, :]).then_inc(S["rows_done"], 1)
                    if k == 3 and group(i - 1):
                        wait(pe, "cols2_ready", i)
                        nc.tensor.transpose(p_rows2[0:NR, :], cols2_part[:].rearrange("p a b c -> p (a b c)"),
                                            ident_bf[:, :]).then_inc(S["rows2_done"], 1)
                    if graph(t - 3):
                        q = (k - 3) % 2
                        project2(h1T_hi[:, q], h1T_lo[:, q], (2, 3)).then_inc(S["xl2_done"], 1)
                    if k == 3 and group(i - 1):
                        wait(pe, "rows2_ready", i)
                        wait(pe, "result_ready", 2 * (i - 1))
                        scores(p_o2, rows2[:, :], neg_mask[:, 1 - par], False).then_inc(S["score2_done"], 1)
                    if k == 1 and group(i - 2):
                        wait(pe, "prob2_ready", i - 1)
                        wait(pe, "probT_ready", capped(t - 1, NB))
                        turn(prob2[:, :]).then_inc(S["turn2_done"], 1)

            run(pe, body)

        @block.vector
        def _(dve):
            def b1_parts():
                dve.wait_ge(S["b1_in"], 48)
                dve.tensor_copy(b1_part[:, 0], b1_raw[:, :]).then_inc(S["b1_step"], 1)
                dve.wait_ge(S["b1_step"], 2)
                dve.tensor_tensor(b1_res[:, 0], b1_raw[:, :], b1_part[:, 0], ALU.subtract).then_inc(S["b1_step"], 1)
                dve.wait_ge(S["b1_step"], 3)
                dve.tensor_copy(b1_part[:, 1], b1_res[:, 0]).then_inc(S["b1_step"], 1)
                dve.wait_ge(S["b1_step"], 4)
                dve.tensor_tensor(b1_part[:, 2], b1_res[:, 0], b1_part[:, 1], ALU.subtract).then_inc(S["b1_step"], 1)
                dve.wait_ge(S["b1_step"], 5)
                dve.wait_ge(S["const_ready"], 6)
                for p in range(3):
                    dve.tensor_copy(b1_rows[32 * p:32 * p + H, :], b1_part[32 * p:32 * p + H, p])\
                       .then_inc(S["b1_ready"], 1)

            def w1_columns():
                n = 0
                for c in range(KC):
                    for side in range(2):
                        dve.wait_ge(S["w1_prod"], n + 1)
                        dve.tensor_reduce(w1[:, c, side, HALF * F:XW],
                                          w_prod[:, n % 2, 0:2, :].rearrange("p a (b f) -> p (a b) f", f=F),
                                          AX.X, ALU.add).then_inc(S["w1_att"], 1)
                        n += 1
                dve.wait_ge(S["w1_att"], 2 * KC)
                dve.tensor_copy(w1_hi[:], w1[:]).then_inc(S["w1_hi_ready"], 1)
                dve.wait_ge(S["w1_hi_ready"], 1)
                dve.tensor_tensor(w1_lo[:], w1[:], w1_hi[:].bitcast(fp32), ALU.subtract).then_inc(S["w1_lo_ready"], 1)

            def w2_columns():
                for side in range(2):
                    dve.wait_ge(S["w2_prod"], side + 1)
                    dve.tensor_reduce(w2[:, :, DO + side], w_prod[:, side], AX.X, ALU.add).then_inc(S["w2_att"], 1)
                dve.wait_ge(S["w2_att"], 2)
                dve.tensor_copy(w2_hi[:], w2[:]).then_inc(S["w2_hi_ready"], 1)
                dve.wait_ge(S["w2_hi_ready"], 1)
                dve.tensor_tensor(w2_lo[:], w2[:], w2_hi[:].bitcast(fp32), ALU.subtract).then_inc(S["w2_lo_ready"], 1)

            def input_stats(b, par, c):
                dve.bn_stats(stats[:, c, :], xs[:, bass.ds(b * D, D)]).then_inc(S["stats_done"], 1)
                wait(dve, "stats_done", b + 1)
                held(dve, b)
                dve.bn_aggr(mean_var[:, par, c, :], stats[:, c, :]).then_inc(S["mv_ready"], 1)

            def normalise_input(b, g, par, c):
                wait(dve, "ln_ready", 2 * (g + 1))
                wait(dve, "hT_done", b - 1)
                dve.tensor_scalar(hn[:, c % 2], xs[:, bass.ds(b * D, D)], neg_mean[:, par, c:c + 1],
                                  rstd[:, par, c:c + 1], ALU.add, ALU.mult).then_inc(S["hn_ready"], 1)

            def leaky_and_top(bank, scaled_t, z_t, minus_top_t, z_name, top_name, z_count):
                dve.tensor_tensor(z_t, bank[:, :], scaled_t, ALU.max).then_inc(S[z_name], 1)
                wait(dve, z_name, z_count)
                dve.tensor_reduce(minus_top_t, slots(z_t), AX.X, ALU.max, negate=True).then_inc(S[top_name], 1)

            def body(i, par, r):
                if isinstance(i, int) and i == -1:
                    dve.memset(b1_raw[:, :], 0.0).then_inc(S["b1_step"], 1)
                for k in range(4):
                    t = 4 * i + k
                    if graph(t + 1):
                        normalise_input(t + 1, i + (k + 1) // 4, (par + (k + 1) // 4) % 2, (k + 1) % 4)
                    if graph(t - 1):
                        b, q = t - 1, (k - 1) % 2
                        wait(dve, "scaled_ready", b + 1)
                        wait(dve, "e_ready", b - 1)
                        leaky_and_top(p_score, scaled[:, q], z[:, q], minus_top[:, q], "z_ready", "top_ready", b + 1)
                    if k == 0 and group(i):
                        if isinstance(i, int) and i == 0:
                            dve.wait_ge(S["ident_ready"], 3)
                        wait(dve, f"adj_in{par}", 16 * (r + 1))
                        wait(dve, "score2_done", i - 1)
                        dve.scalar_tensor_tensor(out=neg_mask[:, par], in0=adj_raw[:, par], scalar=0.0,
                                                 in1=off_diag_neg[:, :].unsqueeze(1).to_broadcast([128, G, N]),
                                                 op0=ALU.is_le, op1=ALU.mult).then_inc(S["mask_ready"], 1)
                    if k == 1 and group(i - 2):
                        wait(dve, "e2_ready", i - 1)
                        wait(dve, "prob2_ready", i - 2)
                        dve.reciprocal(rden2[:, :], den2[:, :]).then_inc(S["rden2_ready"], 1)
                    if graph(t + 1):
                        wait(dve, "hT_hi_ready", t + 2)
                        wait(dve, "xl_done", t)
                        dve.scalar_tensor_tensor(out=hT_lo[:, (k + 1) % 2].rearrange("p c n -> p (c n)"), in0=p_hT[:, 0:D],
                                                 scalar=0.0,
                                                 in1=hT_hi[:, (k + 1) % 2].rearrange("p c n -> p (c n)").bitcast(fp32),
                                                 op0=ALU.max, op1=ALU.subtract).then_inc(S["hT_lo_ready"], 1)
                    if k == 0 and group(i - 2):
                        wait(dve, "scaled2_ready", i - 1)
                        wait(dve, "e2_ready", i - 2)
                        leaky_and_top(p_o2, scaled2[:, :], z2[:, :], minus_top2[:, :], "z2_ready", "top2_ready", i - 1)
                    if k in (2, 3) and group(i - 2):
                        j, pair = i - 2, k - 2
                        wait(dve, "o2_done", 2 * j + pair + 1)
                        wait(dve, f"stored{pair}", 16 * j)
                        wait(dve, "xb_ready", G * j + 2 * pair + 2)
                        dve.tensor_tensor(result[:, pair].rearrange("p b d -> p (b d)"), p_o2[:, :],
                                          xs[:, bass.ds((G * j + 2 * pair) * D, 2 * D)], ALU.add)\
                           .then_inc(S["result_ready"], 1)
                    for c in ((0, 1), (2,), (3,), ())[k]:
                        if group(i + 1):
                            g = i + 1
                            if c == 0:
                                wait(dve, f"x_in{1 - par}", 16 * (r + 1 + par))
                                wait(dve, "ln_ready", 2 * (g - 1))
                            wait(dve, "mv_ready", G * (g - 1) + c + 1)
                            input_stats(G * g + c, 1 - par, c)
                    if graph(t - 1):
                        b, q = t - 1, (k - 1) % 2
                        wait(dve, "e_ready", b + 1)
                        wait(dve, "prob_ready", b - 1)
                        dve.reciprocal(rden[:, q], den[:, q]).then_inc(S["rden_ready"], 1)
                    if graph(t - 2):
                        b, q = t - 2, k % 2
                        wait(dve, "eexp_ready", b + 1)
                        wait(dve, "h1T_ready", b - 1)
                        dve.tensor_scalar(elu_low[:, q], elu_exp[:, q], 1.0, -1.0, ALU.min, ALU.add)\
                           .then_inc(S["elow_done"], 1)
                        wait(dve, "elow_done", b + 1)
                        wait(dve, "h1T_lo_ready", b - 1)
                        dve.tensor_tensor(h1T[:, q], p_o1[:, :], elu_low[:, q], ALU.max).then_inc(S["h1T_ready"], 1)
                        wait(dve, "h1T_ready", b + 1)
                        wait(dve, "xl2_done", b - 1)
                        dve.tensor_copy(h1T_hi[:, q], h1T[:, q]).then_inc(S["h1T_hi_ready"], 1)
                    if isinstance(i, int) and i == -1 and k == 3:
                        w1_columns()
                    if isinstance(i, int) and i == 0 and k == 0:
                        b1_parts()
                        w2_columns()

            run(dve, body)


_INS = ['x', 'adj', 'L0_gnn_W1', 'L0_gnn_att_src1', 'L0_gnn_att_dst1', 'L0_gnn_b1', 'L0_gnn_W2', 'L0_gnn_att_src2',
        'L0_gnn_att_dst2', 'L0_gnn_b2']
_OUTS = [((64, 128, 256), 'float32')]


def kernel(**inputs):
    import numpy as _np
    import concourse.bacc as _bacc
    from concourse import mybir as _mybir
    from concourse.bass_utils import run_bass_kernel_spmd as _run

    nc = _bacc.Bacc("TRN2", target_bir_lowering=False, num_devices=1)
    arrays, args = {}, []
    for name in _INS:
        a = _np.ascontiguousarray(inputs[name])
        arrays[f"in_{name}_dram"] = a
        args.append(nc.dram_tensor(f"in_{name}_dram", a.shape, _mybir.dt.from_np(a.dtype), kind="ExternalInput").ap())
    for i, (shape, dtype) in enumerate(_OUTS):
        dt = _mybir.dt.from_np(_np.dtype(dtype))
        args.append(nc.dram_tensor(f"out_{i}_dram", shape, dt, kind="ExternalOutput").ap())
    preln_gat_residual_kernel(nc, *args)
    r = _run(nc, [arrays], core_ids=[0])
    got = tuple(r.results[0][f"out_{i}_dram"] for i in range(len(_OUTS)))
    return got[0]
```

```python
import concourse.bass as bass
from concourse import mybir
from contextlib import ExitStack


def preln_gat_residual_kernel(nc: bass.Bass, x, adj, W1, att_src1, att_dst1, b1, W2, att_src2, att_dst2, b2, out):
    fp32, bf16, i32 = mybir.dt.float32, mybir.dt.bfloat16, mybir.dt.int32
    fp32r = mybir.dt.float32r
    ALU = mybir.AluOpType
    ACT = mybir.ActivationFunctionType
    AX = mybir.AxisListType

    NB, N, D = x.shape
    H, F = att_src1.shape
    DO = W2.shape[1]
    G = 4
    NG = NB // G
    KC = D // 128
    HALF = H // 2
    XW = HALF * F + H
    YW = DO + 2
    U = G * N
    NR = 12
    NEG = -float(2 ** 60)
    SLOPE = 0.2
    EPS = 1e-5
    assert H == G and N == 128 and F == 128 and D == 256 and DO == D

    ctx = ExitStack()
    with ctx:
        def sb(name, shape, dt=fp32):
            return ctx.enter_context(nc.sbuf_tensor(name, shape, dt))

        def pb(name, shape, dt=fp32):
            return ctx.enter_context(nc.psum_tensor(name, shape, dt))

        def sem(name):
            return ctx.enter_context(nc.semaphore(name))

        ident = sb("ident", [128, 128])
        ident_bf = sb("ident_bf", [128, 128], bf16)
        off_diag_neg = sb("off_diag_neg", [128, 128])
        pick_src = sb("pick_src", [NR, 4, 128], bf16)
        w1 = sb("w1", [128, KC, 2, XW])
        w1_hi = sb("w1_hi", [128, KC, 2, XW], fp32r)
        w1_lo = sb("w1_lo", [128, KC, 2, XW], fp32r)
        w2 = sb("w2", [128, H, YW])
        w2_hi = sb("w2_hi", [128, H, YW], fp32r)
        w2_lo = sb("w2_lo", [128, H, YW], fp32r)
        a1_all = sb("a1_all", [128, 2, H, F])
        a2_all = sb("a2_all", [128, 2, DO])
        w_prod = sb("w_prod", [128, 2, 4, 256])
        w2_prod = sb("w2_prod", [128, 2, H, DO])
        b1_all = sb("b1_all", [128, 2, XW])
        b2_all = sb("b2_all", [128, DO])
        minus_half = sb("minus_half", [128, G])
        xs = sb("xs", [128, NB * D])
        adj_raw = sb("adj_raw", [128, 2, G, N], i32)
        neg_mask = sb("neg_mask", [128, 2, G, N], bf16)
        stats = sb("stats", [128, 2, G, 6])
        mean_var = sb("mean_var", [128, 2, G, 2])
        var_eps = sb("var_eps", [128, G])
        rstd = sb("rstd", [128, 2, G])
        neg_mean = sb("neg_mean", [128, G])
        shift = sb("shift", [128, 2, G])
        hn = sb("hn", [128, 2, D])
        hT_hi = sb("hT_hi", [128, 2, KC, N], fp32r)
        hT_lo = sb("hT_lo", [128, 2, KC, N], fp32r)
        xl = sb("xl", [128, 4, 2, XW])
        cols_res = sb("cols_res", [128, 4])
        cols_part = sb("cols_part", [128, 2, 3, 4], bf16)
        rows = sb("rows", [NR, 2, N], bf16)
        score = sb("score", [128, 2, U])
        z = sb("z", [128, 2, U])
        minus_top = sb("minus_top", [128, 2, 4])
        e = sb("e", [128, 2, U])
        den = sb("den", [128, 2, 4])
        rden = sb("rden", [128, 2, 4])
        prob = sb("prob", [128, 2, U])
        probT = sb("probT", [128, 2, U])
        elu_exp = sb("elu_exp", [128, 2, U])
        elu_low = sb("elu_low", [128, 2, U])
        h1T = sb("h1T", [128, 2, U])
        h1T_hi = sb("h1T_hi", [128, 2, U], fp32r)
        h1T_lo = sb("h1T_lo", [128, 2, U], fp32r)
        xl2 = sb("xl2", [128, 2, G, YW])
        cols2_res = sb("cols2_res", [128, 4])
        cols2_part = sb("cols2_part", [128, 3, 4], bf16)
        rows2 = sb("rows2", [NR, N], bf16)
        score2 = sb("score2", [128, U])
        z2 = sb("z2", [128, U])
        minus_top2 = sb("minus_top2", [128, 4])
        e2 = sb("e2", [128, U])
        den2 = sb("den2", [128, 4])
        rden2 = sb("rden2", [128, 4])
        prob2 = sb("prob2", [128, U])
        prob2T = sb("prob2T", [128, U])
        result = sb("result", [128, 2, 2, DO])
        p_hT = pb("p_hT", [128, 512])
        p_xl = pb("p_xl", [128, 2, 512])
        p_score = pb("p_score", [128, 512])
        p_turn = pb("p_turn", [128, 512])
        p_o1 = pb("p_o1", [128, 512])
        p_xl2 = pb("p_xl2", [128, 512])
        p_o2 = pb("p_o2", [128, 512])
        p_rows = p_xl[:, 0, 448:512].bitcast(bf16)
        p_rows2 = p_xl[:, 1, 448:512].bitcast(bf16)

        S = {name: sem(name) for name in (
            "x_in0", "x_in1", "adj_in0", "adj_in1", "w1_in", "w2_in", "b1_in", "b2_in", "stored0", "stored1",
            "const_ready", "ident_ready", "pick_ready", "w1_prod", "w1_att", "w2_prod", "w2_att", "b1_zero",
            "stats_done", "mv_ready", "veps_done", "ln_ready", "hn_ready", "xb_ready", "mask_ready",
            "w1_own", "w1_cols_hi", "w1_hi_ready", "w1_lo_ready", "w2_hi_ready", "w2_lo_ready",
            "hT_done", "hT_hi_ready", "hT_lo_ready", "h1T_hi_ready", "h1T_lo_ready", "xl_done", "xl_ready",
            "cols_step", "cols_ready", "rows_done", "rows_ready",
            "score_done", "score_ready", "z_ready", "top_ready", "e_ready", "rden_ready",
            "prob_ready", "turn_done", "probT_ready", "o1_done", "eexp_ready", "elow_done", "h1T_ready",
            "xl2_done", "xl2_ready", "cols2_step", "cols2_ready", "rows2_done", "rows2_ready",
            "score2_done", "score2_ready", "z2_ready", "top2_ready", "e2_ready",
            "rden2_ready", "prob2_ready", "turn2_done", "prob2T_ready", "o2_done", "result_ready")}

        def wait(eng, name, count):
            if not (isinstance(count, int) and count <= 0):
                eng.wait_ge(S[name], count)

        def held(eng, count):
            if not isinstance(count, int):
                eng.nop(nofuse=True)

        def graph(b):
            return not isinstance(b, int) or 0 <= b < NB

        def group(g):
            return not isinstance(g, int) or 0 <= g < NG

        def capped(v, top_value):
            return min(v, top_value) if isinstance(v, int) else v

        def at(i, par, k, behind):
            b, d = 4 * i + k - behind, (k - behind) // 4
            return (b, (k - behind) % 4, i + d, (par + d) % 2) if graph(b) else None

        def slots(ap):
            return ap.rearrange("p (a n) -> p a n", a=4)

        FIRST, LAST = -2, NG - 1 + 3
        FULL = range(4, NG - 4)

        def run(eng, body):
            for i in range(FIRST, FULL.start):
                body(i, i % 2, None)
            with eng.Fori(FULL.start // 2, FULL.stop // 2) as r:
                body(2 * r, 0, r)
                body(2 * r + 1, 1, r)
            for i in range(FULL.stop, LAST + 1):
                body(i, i % 2, None)

        def loads(g, par, r, gp, ahead):
            return g // 2 + 1 if isinstance(g, int) else r + (par + ahead - gp) // 2 + 1

        def w1_times(eng, c, side):
            return eng.tensor_tensor(w_prod[:, c, 2 * side:2 * side + 2, :], w1[:, c, :, 0:HALF * F],
                                     a1_all[:, side].rearrange("p (a b) f -> p a (b f)", a=2), ALU.mult)

        block = ctx.enter_context(nc.Block())

        @block.sync
        def _(sp):
            def load_x(g, par):
                sp.dma_start(xs[:, bass.ds(g * G * D, G * D)].rearrange("p (b d) -> p b d", b=G),
                             x[bass.ds(g * G, G)].rearrange("b p d -> p b d")).then_inc(S[f"x_in{par}"], 16)

            def load_adj(g, par):
                sp.dma_start(adj_raw[:, par], adj[bass.ds(g * G, G)].rearrange("b s d -> s b d"))\
                  .then_inc(S[f"adj_in{par}"], 16)

            def body(i, par, r):
                if group(i + 3) and (not isinstance(i, int) or i >= -1):
                    wait(sp, "stats_done", G * (i + 2))
                    load_x(i + 3, 1 - par)
                if group(i + 2) and (not isinstance(i, int) or i >= 0):
                    wait(sp, "mask_ready", i + 1)
                    load_adj(i + 2, par)
                j = i - 2
                if group(j):
                    for pair in range(2):
                        wait(sp, "result_ready", 2 * j + pair + 1)
                        sp.dma_start(out[bass.ds(j * G + 2 * pair, 2)].rearrange("b p d -> p b d"),
                                     result[:, pair]).then_inc(S[f"stored{pair}"], 16)

            load_x(0, 0)
            for c in range(KC):
                for half in range(2):
                    sp.dma_start(w1[:, c, half, 0:HALF * F],
                                 W1[c * 128:(c + 1) * 128, half * HALF * F:(half + 1) * HALF * F])\
                      .then_inc(S["w1_in"], 16)
            load_adj(0, 0)
            load_x(1, 1)
            load_adj(1, 1)
            sp.dma_start(b1_all[:, :, 0:HALF * F],
                         b1.rearrange("(a f) -> a f", a=2).partition_broadcast(128)).then_inc(S["b1_in"], 16)
            for side, a in enumerate((att_src2, att_dst2)):
                sp.dma_start(a2_all[:, side], a.rearrange("a o -> (a o)").partition_broadcast(128))\
                  .then_inc(S["w2_in"], 16)
            sp.dma_start(w2[:, :, 0:DO], W2.rearrange("(h f) o -> f h o", h=H)).then_inc(S["w2_in"], 16)
            sp.dma_start(b2_all[:, :], b2.partition_broadcast(128)).then_inc(S["b2_in"], 16)

            run(sp, body)
            wait(sp, "stored0", 16 * NG)
            wait(sp, "stored1", 16 * NG)

        @block.gpsimd
        def _(pool):
            def small_constants():
                pool.memset(ident[:, :], 0.0).then_inc(S["const_ready"], 1)
                pool.memset(minus_half[:, :], -0.5).then_inc(S["const_ready"], 1)
                pool.wait_ge(S["const_ready"], 2)
                pool.affine_select(out=ident[:, :], in_=ident[:, :], compare_op=ALU.not_equal, fill=1.0,
                                   base=0, pattern=[[-1, 128]], channel_multiplier=1).then_inc(S["ident_ready"], 1)
                pool.wait_ge(S["ident_ready"], 1)
                pool.tensor_copy(ident_bf[:, :], ident[:, :]).then_inc(S["ident_ready"], 1)
                pool.tensor_scalar(off_diag_neg[:, :], ident[:, :], -NEG, NEG, ALU.mult, ALU.add)\
                    .then_inc(S["ident_ready"], 1)

            def pick_matrices():
                pool.memset(pick_src[:], 0.0).then_inc(S["const_ready"], 1)
                pool.wait_ge(S["const_ready"], 3)
                for p in range(3):
                    if p:
                        pool.wait_ge(S["pick_ready"], p)
                    pool.affine_select(out=pick_src[:], in_=pick_src[:], compare_op=ALU.not_equal, fill=1.0,
                                       base=-4 * p, pattern=[[-1, 4], [0, 128]],
                                       channel_multiplier=1).then_inc(S["pick_ready"], 1)

            def w1_product():
                pool.wait_ge(S["w1_in"], 16 * (2 * KC + 2))
                w1_times(pool, 1, 0).then_inc(S["w1_prod"], 1)

            def w1_low():
                feats = slice(0, HALF * F)
                pool.wait_ge(S["w1_hi_ready"], 1)
                pool.tensor_tensor(w1_lo[:, :, :, feats], w1[:, :, :, feats], w1_hi[:, :, :, feats].bitcast(fp32),
                                   ALU.subtract).then_inc(S["w1_lo_ready"], 1)

            def w2_product(side):
                pool.wait_ge(S["w2_in"], 16 * 3)
                pool.tensor_tensor(w2_prod[:, side], w2[:, :, 0:DO],
                                   a2_all[:, side].unsqueeze(1).to_broadcast([128, 4, DO]),
                                   ALU.mult).then_inc(S["w2_prod"], 1)

            def layernorm_terms(g, par):
                wait(pool, "mv_ready", g + 1)
                wait(pool, "hn_ready", G * (g - 1))
                held(pool, g)
                pool.tensor_scalar(var_eps[:, :], mean_var[:, par, :, 1], EPS, 0.0, ALU.add, ALU.add)\
                    .then_inc(S["veps_done"], 1)
                pool.tensor_scalar(neg_mean[:, :], mean_var[:, par, :, 0], -1.0, 0.0, ALU.mult, ALU.add)\
                    .then_inc(S["veps_done"], 1)
                wait(pool, "veps_done", 2 * g + 2)
                pool.tensor_tensor(rstd[:, par], var_eps[:, :], minus_half[:, :], ALU.pow)\
                    .then_inc(S["ln_ready"], 1)
                wait(pool, "ln_ready", 2 * g + 1)
                pool.tensor_tensor(shift[:, par], neg_mean[:, :], rstd[:, par], ALU.mult)\
                    .then_inc(S["ln_ready"], 1)

            def split(src, res, part, done, first, last_name):
                held(pool, done)
                pool.tensor_copy(part[:, 0], src).then_inc(S[first], 1)
                wait(pool, first, done + 1)
                pool.tensor_tensor(res, src, part[:, 0], ALU.subtract).then_inc(S[first], 1)
                wait(pool, first, done + 2)
                held(pool, done)
                pool.tensor_copy(part[:, 1], res).then_inc(S[first], 1)
                wait(pool, first, done + 3)
                pool.tensor_tensor(part[:, 2], res, part[:, 1], ALU.subtract).then_inc(S[last_name], 1)

            def scale(dst, src, r, name):
                pool.tensor_tensor(slots(dst), slots(src), r.unsqueeze(2).to_broadcast([128, 4, 128]), ALU.mult)\
                    .then_inc(S[name], 1)

            def body(i, par, r):
                for k in range(4):
                    if k == 3 and group(i - 2):
                        g = i - 2
                        wait(pool, "rden2_ready", g + 1)
                        wait(pool, "turn2_done", g)
                        scale(prob2[:, :], e2[:, :], rden2[:, :], "prob2_ready")
                    if here := at(i, par, k, 0):
                        b, c = here[:2]
                        q = c % 2
                        wait(pool, "xl_ready", b + 1)
                        wait(pool, "rows_done", b - 1)
                        split(xl[:, c, 0, HALF * F:XW], cols_res[:, :], cols_part[:, q], 3 * b,
                              "cols_step", "cols_ready")
                    if here := at(i, par, k, 2):
                        b, c = here[:2]
                        q = c % 2
                        wait(pool, "rden_ready", b + 1)
                        wait(pool, "turn_done", b - 1)
                        scale(prob[:, q], e[:, q], rden[:, q], "prob_ready")
                    if k == 0 and group(i - 2):
                        g, gp = i - 2, par
                        wait(pool, "xl2_ready", G * (g + 1))
                        wait(pool, "rows2_done", g)
                        split(xl2[:, gp, :, DO], cols2_res[:, :], cols2_part[:],
                              3 * g, "cols2_step", "cols2_ready")
                    if here := at(i, par, k, 4):
                        b, c = here[:2]
                        q = c % 2
                        wait(pool, "h1T_hi_ready", b + 1)
                        wait(pool, "xl2_done", b - 1)
                        pool.tensor_tensor(h1T_lo[:, q], h1T[:, q], h1T_hi[:, q].bitcast(fp32), ALU.subtract)\
                            .then_inc(S["h1T_lo_ready"], 1)
                    if here := at(i, par, k, 6):
                        b = here[0]
                        if isinstance(b, int) and b == 0:
                            pool.wait_ge(S["b2_in"], 16)
                        wait(pool, "hn_ready", b + 1)
                        xb = xs[:, bass.ds(b * D, D)]
                        pool.tensor_tensor(xb, xb, b2_all[:, :], ALU.add).then_inc(S["xb_ready"], 1)
                    if k == 0 and group(i + 1):
                        g, gp = i + 1, 1 - par
                        layernorm_terms(g, gp)
                    if isinstance(i, int) and k == 0 and i == -1:
                        w1_product()
                        w1_low()
                        w2_product(0)
                        w2_product(1)

            small_constants()
            pick_matrices()
            run(pool, body)

        @block.scalar
        def _(act):
            for side, a in enumerate((att_src1, att_dst1)):
                act.dma_start(a1_all[:, side], a.partition_broadcast(128)).then_inc(S["w1_in"], 16)
            act.wait_ge(S["w1_in"], 16 * (2 * KC + 2))
            act.activation(w1_hi[:, :, :, 0:HALF * F], w1[:, :, :, 0:HALF * F], ACT.Copy).then_inc(S["w1_hi_ready"], 1)

            def add_terms(dst, bank, terms):
                for a in range(4):
                    its = slice(a * 128, (a + 1) * 128)
                    last = act.activation(dst[:, its], bank[:, its], ACT.Identity, bias=terms[:, a:a + 1])
                return last

            def exponentials(e_t, z_t, minus_top_t, den_t):
                for a in range(4):
                    its = slice(a * 128, (a + 1) * 128)
                    last = act.activation(e_t[:, its], z_t[:, its], ACT.Exp, bias=minus_top_t[:, a:a + 1],
                                          accum_out=den_t[:, a:a + 1])
                return last

            def body(i, par, r):
                for k in range(4):
                    if here := at(i, par, k, 1):
                        b, c = here[:2]
                        q = c % 2
                        wait(act, "score_done", b + 1)
                        wait(act, "xl_ready", b + 1)
                        wait(act, "z_ready", b - 1)
                        add_terms(score[:, q], p_score, xl[:, c, 1, HALF * F:XW]).then_inc(S["score_ready"], 1)
                    if here := at(i, par, k, -2):
                        b, c = here[:2]
                        q = c % 2
                        wait(act, "hT_done", b + 1)
                        wait(act, "xl_done", b - 1)
                        act.activation(hT_hi[:, q], p_hT[:, 0:D].rearrange("p (n m) -> p n m", n=KC), ACT.Relu)\
                           .then_inc(S["hT_hi_ready"], 1)
                    if here := at(i, par, k, 5):
                        b, c, g, gp = here
                        wait(act, "xl2_done", b + 1)
                        wait(act, "o2_done", 2 * (g - 1))
                        act.activation(xl2[:, gp, c, :], p_xl2[:, 0:YW], ACT.Copy).then_inc(S["xl2_ready"], 1)
                    if here := at(i, par, k, 0):
                        b, c = here[:2]
                        q = c % 2
                        wait(act, "rows_done", b + 1)
                        wait(act, "score_done", b - 1)
                        act.activation(rows[:, q], p_rows[0:NR, :], ACT.Copy).then_inc(S["rows_ready"], 1)
                    if k == 2 and group(i - 2):
                        g = i - 2
                        wait(act, "top2_ready", g + 1)
                        wait(act, "prob2_ready", g)
                        exponentials(e2[:, :], z2[:, :], minus_top2[:, :], den2[:, :]).then_inc(S["e2_ready"], 1)
                    if k == 0 and group(i - 2):
                        g = i - 2
                        wait(act, "rows2_done", g + 1)
                        wait(act, "score2_done", g)
                        act.activation(rows2[:, :], p_rows2[0:NR, :], ACT.Copy).then_inc(S["rows2_ready"], 1)
                    if here := at(i, par, k, 3):
                        b, c = here[:2]
                        q = c % 2
                        wait(act, "o1_done", b + 1)
                        wait(act, "elow_done", b - 1)
                        act.activation(elu_exp[:, q], p_o1[:, :], ACT.Exp).then_inc(S["eexp_ready"], 1)
                    if here := at(i, par, k, 2):
                        b, c = here[:2]
                        q = c % 2
                        wait(act, "turn_done", b + 1)
                        wait(act, "o1_done", b - 1)
                        act.activation(probT[:, q], p_turn[:, :], ACT.Copy).then_inc(S["probT_ready"], 1)
                    if here := at(i, par, k, 1):
                        b, c = here[:2]
                        q = c % 2
                        wait(act, "top_ready", b + 1)
                        wait(act, "prob_ready", b - 1)
                        exponentials(e[:, q], z[:, q], minus_top[:, q], den[:, q]).then_inc(S["e_ready"], 1)
                    if k == 0 and group(i - 2):
                        g, gp = i - 2, par
                        wait(act, "score2_done", g + 1)
                        wait(act, "z2_ready", g)
                        add_terms(score2[:, :], p_o2, xl2[:, gp, :, DO + 1]).then_inc(S["score2_ready"], 1)

            run(act, body)

        @block.tensor
        def _(pe):
            def scores(bank, bank_rows, mask_part, one_mask):
                if one_mask:
                    nc.tensor.matmul(bank[:, :], mask_part, ident_bf[:, :].unsqueeze(1).to_broadcast([128, 4, 128]),
                                     start=True, stop=False)
                for a in range(4):
                    if not one_mask:
                        nc.tensor.matmul(bank[:, a * 128:(a + 1) * 128], mask_part[:, a, :], ident_bf[:, :],
                                         start=True, stop=False)
                    mm = nc.tensor.matmul(bank[:, a * 128:(a + 1) * 128], pick_src[:, a, :], bank_rows,
                                          start=False, stop=(a == 3 or not one_mask))
                return mm

            def project1(hi, lo):
                for c in range(KC):
                    for n, (h_t, w) in enumerate(((hi, w1_hi), (hi, w1_lo), (lo, w1_hi))):
                        for half in range(2):
                            mm = nc.tensor.matmul(p_xl[:, half, 0:XW], h_t[:, c, :], w[:, c, half, :],
                                                  start=(c == 0 and n == 0), stop=(c == KC - 1 and n == 2))
                return mm

            def project2(hi, lo, heads):
                for h in heads:
                    for n, (h_t, w) in enumerate(((hi, w2_hi), (hi, w2_lo), (lo, w2_hi))):
                        mm = nc.tensor.matmul(p_xl2[:, 0:YW], h_t[:, h * 128:(h + 1) * 128], w[:, h, :],
                                              start=(h == 0 and n == 0), stop=(h == H - 1 and n == 2))
                return mm

            def turn(src):
                for a in range(4):
                    mm = nc.tensor.transpose(p_turn[:, a * 128:(a + 1) * 128], src[:, a * 128:(a + 1) * 128],
                                             ident[:, :])
                return mm

            def project_pair(pair, gp):
                for a in (2 * pair, 2 * pair + 1):
                    mm = nc.tensor.matmul(p_o2[:, (a % 2) * DO:(a % 2 + 1) * DO],
                                          prob2T[:, a * 128:(a + 1) * 128], xl2[:, gp, a, 0:DO],
                                          start=True, stop=True)
                return mm

            def body(i, par, r):
                for k in range(4):
                    if here := at(i, par, k, 0):
                        b, c = here[:2]
                        q = c % 2
                        if isinstance(b, int) and b == 0:
                            pe.wait_ge(S["w1_lo_ready"], 2)
                        wait(pe, "hT_lo_ready", b + 1)
                        wait(pe, "xl_ready", b)
                        wait(pe, "rows_ready", b)
                        if k == 1 and group(i - 2):
                            wait(pe, "rows2_ready", i - 1)
                        project1(hT_hi[:, q], hT_lo[:, q]).then_inc(S["xl_done"], 1)
                    if here := at(i, par, k, 1):
                        b, c, g, gp = here
                        q = c % 2
                        if isinstance(b, int) and b == 0:
                            pe.wait_ge(S["pick_ready"], 3)
                        wait(pe, "rows_ready", b + 1)
                        wait(pe, "mask_ready", g + 1)
                        wait(pe, "score_ready", b)
                        scores(p_score, rows[:, q], neg_mask[:, gp, c, :], True).then_inc(S["score_done"], 1)
                    if k == 0 and group(i - 3):
                        g, gp = i - 3, 1 - par
                        wait(pe, "prob2T_ready", g + 1)
                        wait(pe, "result_ready", 2 * g)
                        project_pair(0, gp).then_inc(S["o2_done"], 1)
                    if here := at(i, par, k, 5):
                        b, c = here[:2]
                        q = c % 2
                        if isinstance(b, int) and b == 0:
                            pe.wait_ge(S["w2_lo_ready"], 1)
                        wait(pe, "h1T_lo_ready", b + 1)
                        wait(pe, "xl2_ready", b)
                        project2(h1T_hi[:, q], h1T_lo[:, q], (0, 1))
                    if here := at(i, par, k, -2):
                        b, c = here[:2]
                        q = c % 2
                        wait(pe, "hn_ready", b + 1)
                        wait(pe, "hT_lo_ready", b)
                        for n in range(KC):
                            mm = nc.tensor.transpose(p_hT[:, n * 128:(n + 1) * 128],
                                                     hn[:, q, n * 128:(n + 1) * 128], ident[:, :])
                        mm.then_inc(S["hT_done"], 1)
                    if k == 3 and group(i - 2):
                        g = i - 2
                        wait(pe, "prob2_ready", g + 1)
                        wait(pe, "probT_ready", capped(4 * i + k - 2, NB))
                        turn(prob2[:, :]).then_inc(S["turn2_done"], 1)
                    if here := at(i, par, k, 5):
                        b, c = here[:2]
                        q = c % 2
                        project2(h1T_hi[:, q], h1T_lo[:, q], (2, 3)).then_inc(S["xl2_done"], 1)
                    if k == 0 and group(i - 3):
                        g, gp = i - 3, 1 - par
                        wait(pe, "result_ready", 2 * g + 1)
                        project_pair(1, gp).then_inc(S["o2_done"], 1)
                    if here := at(i, par, k, 0):
                        b, c = here[:2]
                        q = c % 2
                        wait(pe, "cols_ready", b + 1)
                        nc.tensor.transpose(p_rows[0:NR, :], cols_part[:, q].rearrange("p a b -> p (a b)"),
                                            ident_bf[:, :]).then_inc(S["rows_done"], 1)
                    if here := at(i, par, k, 3):
                        b, c = here[:2]
                        q = c % 2
                        wait(pe, "h1T_ready", b)
                        wait(pe, "probT_ready", b + 1)
                        wait(pe, "xl_ready", b + 1)
                        for h in range(H):
                            mm = nc.tensor.matmul(p_o1[:, h * 128:(h + 1) * 128],
                                                  xl[:, c, h // HALF, (h % HALF) * F:(h % HALF + 1) * F],
                                                  probT[:, q, h * 128:(h + 1) * 128], start=True, stop=True)
                        mm.then_inc(S["o1_done"], 1)
                    if k == 0 and group(i - 2):
                        g = i - 2
                        wait(pe, "cols2_ready", g + 1)
                        wait(pe, "xl_ready", capped(4 * i + k + 1, NB))
                        nc.tensor.transpose(p_rows2[0:NR, :], cols2_part[:].rearrange("p a b -> p (a b)"),
                                            ident_bf[:, :]).then_inc(S["rows2_done"], 1)
                    if here := at(i, par, k, 2):
                        b, c = here[:2]
                        q = c % 2
                        wait(pe, "prob_ready", b + 1)
                        wait(pe, "probT_ready", b)
                        if k == 3 and group(i - 2):
                            wait(pe, "prob2T_ready", i - 1)
                        turn(prob[:, q]).then_inc(S["turn_done"], 1)
                    if k == 0 and group(i - 2):
                        g, gp = i - 2, par
                        wait(pe, "rows2_ready", g + 1)
                        wait(pe, "result_ready", 2 * g)
                        scores(p_o2, rows2[:, :], neg_mask[:, gp], False).then_inc(S["score2_done"], 1)

            pe.wait_ge(S["ident_ready"], 3)
            run(pe, body)

        @block.vector
        def _(dve):
            own_quarters = ((0, 1), (1, 1), (0, 0))

            def w1_products():
                dve.wait_ge(S["w1_in"], 16 * (2 * KC + 2))
                for c, side in own_quarters:
                    w1_times(dve, c, side).then_inc(S["w1_own"], 1)

            def w1_sum(c, side):
                dve.tensor_reduce(w1[:, c, side, HALF * F:XW],
                                  w_prod[:, c, 2 * side:2 * side + 2].rearrange("p a (b f) -> p (a b) f", f=F),
                                  AX.X, ALU.add).then_inc(S["w1_att"], 1)

            def first_w1_sums():
                for n, (c, side) in enumerate(own_quarters[0:2]):
                    dve.wait_ge(S["w1_own"], n + 1)
                    w1_sum(c, side)

            def last_w1_sums():
                cols = slice(HALF * F, XW)
                dve.wait_ge(S["w1_own"], 3)
                w1_sum(*own_quarters[2])
                dve.wait_ge(S["w1_prod"], 1)
                w1_sum(1, 0)
                dve.wait_ge(S["w1_att"], 2 * KC)
                dve.tensor_copy(w1_hi[:, :, :, cols], w1[:, :, :, cols]).then_inc(S["w1_cols_hi"], 1)
                dve.wait_ge(S["w1_cols_hi"], 1)
                dve.tensor_tensor(w1_lo[:, :, :, cols], w1[:, :, :, cols], w1_hi[:, :, :, cols].bitcast(fp32),
                                  ALU.subtract).then_inc(S["w1_lo_ready"], 1)

            def w2_column(side):
                dve.wait_ge(S["w2_prod"], side + 1)
                dve.tensor_reduce(w2[:, :, DO + side], w2_prod[:, side], AX.X, ALU.add).then_inc(S["w2_att"], 1)

            def w2_split():
                dve.wait_ge(S["w2_att"], 2)
                dve.tensor_copy(w2_hi[:], w2[:]).then_inc(S["w2_hi_ready"], 1)
                dve.wait_ge(S["w2_hi_ready"], 1)
                dve.tensor_tensor(w2_lo[:], w2[:], w2_hi[:].bitcast(fp32), ALU.subtract).then_inc(S["w2_lo_ready"], 1)

            def aggregate(g, gp):
                held(dve, g)
                for c in range(G):
                    last = dve.bn_aggr(mean_var[:, gp, c, :], stats[:, gp, c, :])
                return last

            def body(i, par, r):
                for k in range(4):
                    if here := at(i, par, k, 0):
                        b, c = here[:2]
                        if isinstance(b, int) and b == 0:
                            dve.wait_ge(S["b1_in"], 16)
                            dve.wait_ge(S["b1_zero"], 1)
                        wait(dve, "xl_done", b + 1)
                        wait(dve, "o1_done", b - 3)
                        dve.tensor_tensor(xl[:, c], p_xl[:, :, 0:XW], b1_all[:], ALU.add).then_inc(S["xl_ready"], 1)
                    if isinstance(i, int) and 4 * i + k == 0:
                        w2_column(0)
                    if isinstance(i, int) and 4 * i + k == 1:
                        w2_column(1)
                    if isinstance(i, int) and 4 * i + k == 3:
                        w2_split()
                    if here := at(i, par, k, 4):
                        b, c = here[:2]
                        q = c % 2
                        wait(dve, "elow_done", b + 1)
                        wait(dve, "h1T_lo_ready", b - 1)
                        dve.tensor_tensor(h1T[:, q], p_o1[:, :], elu_low[:, q], ALU.max).then_inc(S["h1T_ready"], 1)
                    if here := at(i, par, k, 2):
                        b, c = here[:2]
                        q = c % 2
                        wait(dve, "e_ready", b + 1)
                        wait(dve, "prob_ready", b - 1)
                        dve.reciprocal(rden[:, q], den[:, q]).then_inc(S["rden_ready"], 1)
                    if k == 0 and group(i - 3):
                        g = i - 3
                        wait(dve, "o2_done", 2 * g + 1)
                        wait(dve, "stored0", 16 * g)
                        wait(dve, "xb_ready", G * g + 2)
                        dve.tensor_tensor(result[:, 0].rearrange("p b d -> p (b d)"), p_o2[:, :],
                                          xs[:, bass.ds((G * g) * D, 2 * D)], ALU.add)\
                           .then_inc(S["result_ready"], 1)
                    if k == 2 and group(i - 2):
                        g = i - 2
                        wait(dve, "z2_ready", g + 1)
                        wait(dve, "e2_ready", g)
                        dve.tensor_reduce(minus_top2[:, :], slots(z2[:, :]), AX.X, ALU.max, negate=True)\
                           .then_inc(S["top2_ready"], 1)
                    if here := at(i, par, k, 4):
                        b, c = here[:2]
                        q = c % 2
                        wait(dve, "h1T_ready", b + 1)
                        wait(dve, "xl2_done", b - 1)
                        dve.tensor_copy(h1T_hi[:, q], h1T[:, q]).then_inc(S["h1T_hi_ready"], 1)
                    if k == 1 and group(i - 2):
                        g = i - 2
                        wait(dve, "score2_ready", g + 1)
                        wait(dve, "e2_ready", g)
                        dve.scalar_tensor_tensor(out=z2[:, :], in0=score2[:, :], scalar=SLOPE, in1=score2[:, :],
                                                 op0=ALU.mult, op1=ALU.max).then_inc(S["z2_ready"], 1)
                    if k == 3 and group(i - 2):
                        g = i - 2
                        wait(dve, "turn2_done", g + 1)
                        wait(dve, "o2_done", 2 * g)
                        dve.tensor_copy(prob2T[:, :], p_turn[:, :]).then_inc(S["prob2T_ready"], 1)
                    if here := at(i, par, k, -3):
                        b, c, g, gp = here
                        q = c % 2
                        wait(dve, "ln_ready", 2 * (g + 1))
                        wait(dve, "hT_done", b - 1)
                        dve.tensor_scalar(hn[:, q], xs[:, bass.ds(b * D, D)], rstd[:, gp, c:c + 1],
                                          shift[:, gp, c:c + 1], ALU.mult, ALU.add).then_inc(S["hn_ready"], 1)
                    if isinstance(i, int) and 4 * i + k == -3:
                        first_w1_sums()
                    if here := at(i, par, k, 1):
                        b, c = here[:2]
                        q = c % 2
                        wait(dve, "score_ready", b + 1)
                        wait(dve, "e_ready", b - 1)
                        dve.scalar_tensor_tensor(out=z[:, q], in0=score[:, q], scalar=SLOPE, in1=score[:, q],
                                                 op0=ALU.mult, op1=ALU.max).then_inc(S["z_ready"], 1)
                    if k == 0 and group(i - 3):
                        g = i - 3
                        wait(dve, "o2_done", 2 * g + 2)
                        wait(dve, "stored1", 16 * g)
                        wait(dve, "xb_ready", G * g + 4)
                        dve.tensor_tensor(result[:, 1].rearrange("p b d -> p (b d)"), p_o2[:, :],
                                          xs[:, bass.ds((G * g + 2) * D, 2 * D)], ALU.add)\
                           .then_inc(S["result_ready"], 1)
                    if k == 0 and group(i + 1):
                        g, gp = i + 1, 1 - par
                        wait(dve, "ln_ready", 2 * (g - 1))
                        wait(dve, "stats_done", G * (g + 1))
                        aggregate(g, gp).then_inc(S["mv_ready"], 1)
                    if isinstance(i, int) and 4 * i + k == -4:
                        w1_products()
                    if here := at(i, par, k, 1):
                        b, c = here[:2]
                        q = c % 2
                        wait(dve, "z_ready", b + 1)
                        wait(dve, "e_ready", b - 1)
                        dve.tensor_reduce(minus_top[:, q], slots(z[:, q]), AX.X, ALU.max, negate=True)\
                           .then_inc(S["top_ready"], 1)
                    if here := at(i, par, k, -2):
                        b, c = here[:2]
                        q = c % 2
                        wait(dve, "hT_hi_ready", b + 1)
                        wait(dve, "xl_done", b - 1)
                        dve.scalar_tensor_tensor(out=hT_lo[:, q].rearrange("p c n -> p (c n)"),
                                                 in0=p_hT[:, 0:D], scalar=0.0,
                                                 in1=hT_hi[:, q].rearrange("p c n -> p (c n)").bitcast(fp32),
                                                 op0=ALU.max, op1=ALU.subtract).then_inc(S["hT_lo_ready"], 1)
                    if isinstance(i, int) and 4 * i + k == -2:
                        last_w1_sums()
                    if k == 2 and group(i - 2):
                        g = i - 2
                        wait(dve, "e2_ready", g + 1)
                        wait(dve, "prob2_ready", g)
                        dve.reciprocal(rden2[:, :], den2[:, :]).then_inc(S["rden2_ready"], 1)
                    if here := at(i, par, k, -8):
                        b, c, g, gp = here
                        if c == 0:
                            wait(dve, f"x_in{gp}", 16 * loads(g, par, r, gp, (k + 8) // 4))
                            wait(dve, "mv_ready", g - 1)
                        dve.bn_stats(stats[:, gp, c, :], xs[:, bass.ds(b * D, D)]).then_inc(S["stats_done"], 1)
                    if k == 0 and group(i):
                        g, gp = i, par
                        if isinstance(g, int) and g == 0:
                            dve.wait_ge(S["ident_ready"], 3)
                        wait(dve, f"adj_in{gp}", 16 * loads(g, par, r, gp, 0))
                        wait(dve, "score2_done", g - 1)
                        dve.scalar_tensor_tensor(out=neg_mask[:, gp], in0=adj_raw[:, gp], scalar=0.0,
                                                 in1=off_diag_neg[:, :].unsqueeze(1).to_broadcast([128, G, N]),
                                                 op0=ALU.is_le, op1=ALU.mult).then_inc(S["mask_ready"], 1)
                    if here := at(i, par, k, 3):
                        b, c = here[:2]
                        q = c % 2
                        wait(dve, "eexp_ready", b + 1)
                        wait(dve, "h1T_ready", b - 1)
                        dve.tensor_scalar(elu_low[:, q], elu_exp[:, q], 1.0, -1.0, ALU.min, ALU.add)\
                           .then_inc(S["elow_done"], 1)

            dve.memset(b1_all[:, :, HALF * F:XW], 0.0).then_inc(S["b1_zero"], 1)
            run(dve, body)


_INS = ['x', 'adj', 'L0_gnn_W1', 'L0_gnn_att_src1', 'L0_gnn_att_dst1', 'L0_gnn_b1', 'L0_gnn_W2', 'L0_gnn_att_src2',
        'L0_gnn_att_dst2', 'L0_gnn_b2']
_OUTS = [((64, 128, 256), 'float32')]


def kernel(**inputs):
    import numpy as _np
    import concourse.bacc as _bacc
    from concourse import mybir as _mybir
    from concourse.bass_utils import run_bass_kernel_spmd as _run

    nc = _bacc.Bacc("TRN2", target_bir_lowering=False, num_devices=1)
    arrays, args = {}, []
    for name in _INS:
        a = _np.ascontiguousarray(inputs[name])
        arrays[f"in_{name}_dram"] = a
        args.append(nc.dram_tensor(f"in_{name}_dram", a.shape, _mybir.dt.from_np(a.dtype), kind="ExternalInput").ap())
    for i, (shape, dtype) in enumerate(_OUTS):
        dt = _mybir.dt.from_np(_np.dtype(dtype))
        args.append(nc.dram_tensor(f"out_{i}_dram", shape, dt, kind="ExternalOutput").ap())
    preln_gat_residual_kernel(nc, *args)
    r = _run(nc, [arrays], core_ids=[0])
    got = tuple(r.results[0][f"out_{i}_dram"] for i in range(len(_OUTS)))
    return got[0]
```
